# Optimizing a Trainium2 kernel written in Bass

```python
import numpy as np
import jax
import jax.numpy as jnp

def _softmax(x, axis=-1):
    return jax.nn.softmax(x, axis=axis)

def _gelu(x):
    return jax.nn.gelu(x, approximate=True)

def _silu(x):
    return jax.nn.silu(x)

def _sigmoid(x):
    return jax.nn.sigmoid(x)

def _layernorm(x, axis=-1, eps=1e-05):
    m = jnp.mean(x, axis=axis, keepdims=True)
    v = jnp.var(x, axis=axis, keepdims=True)
    return (x - m) / jnp.sqrt(v + eps)

def _scatter_add(tgt, idx, src, axis=0):
    return tgt.at[idx].add(src)

def _segment_sum(src, seg, n):
    return jax.ops.segment_sum(src, seg, n)
kernel_name = 'mk_conv_seq_d4_conv_nchw512_r2_d4b286'

def setup_inputs(seed: int=0):
    np.random.seed(seed)
    _w = jnp.asarray

    def _rec_inputs():
        import jax
        import jax.numpy as jnp
        _gk = jax.random.key(seed)
        x = -0.0005207 + 1.001 * jax.random.normal(jax.random.fold_in(_gk, 1), (1, 256, 32, 32), jnp.float32)
        return x
    x = _rec_inputs()

    def _L0_conv_setup():
        import jax, jax.numpy as jnp
        import numpy as np
        CH = 256
        HEADS = 8
        REDUCTION = 2
        INNER = max(CH // REDUCTION, HEADS)
        POS_RES = 16
        LN_EPS = 1e-05
        key = jax.random.key(seed)
        ks = jax.random.split(key, 7)
        B, H, W = (1, 32, 32)
        x = jax.random.normal(ks[0], (B, CH, H, W), dtype=jnp.float32)
        w_qkv = jax.random.normal(ks[1], (INNER * 3, CH), dtype=jnp.float32) * 0.02
        w_proj = jax.random.normal(ks[2], (CH, INNER), dtype=jnp.float32) * 0.02
        b_proj = jnp.zeros((CH,), dtype=jnp.float32)
        pos_bias = jax.random.normal(ks[3], (1, HEADS, POS_RES, POS_RES), dtype=jnp.float32) * 0.02
        gamma = jnp.ones((CH,), dtype=jnp.float32)
        beta = jnp.zeros((CH,), dtype=jnp.float32)
        return {'x': x, 'w_qkv': w_qkv, 'w_proj': w_proj, 'b_proj': b_proj, 'pos_bias': pos_bias, 'gamma': gamma, 'beta': beta}
    _L0_conv_all = _L0_conv_setup()
    _L0_conv_in = {k: v for k, v in _L0_conv_all.items() if k in ('w_qkv', 'w_proj', 'b_proj', 'pos_bias', 'gamma', 'beta')}
    del _L0_conv_all

    def _L1_conv_setup():
        import jax, jax.numpy as jnp
        import numpy as np
        import math
        HEADS = 8
        DIM_HEAD = 32
        EMB = 256
        GROUPS = 32
        EPS = 100000.0
        key = jax.random.key(seed)
        ks = jax.random.split(key, 11)
        B, D, H, W = (2, EMB, 32, 32)
        s = 1.0 / math.sqrt(EMB)
        inp = {'input': jax.random.normal(ks[0], (B, D, H, W), dtype=jnp.float32), 'gn_gamma': jnp.ones((EMB,), dtype=jnp.float32), 'gn_beta': jnp.zeros((EMB,), dtype=jnp.float32), 'wq': jax.random.normal(ks[1], (EMB, EMB), dtype=jnp.float32) * s, 'bq': jax.random.normal(ks[2], (EMB,), dtype=jnp.float32) * 0.01, 'wk': jax.random.normal(ks[3], (EMB, EMB), dtype=jnp.float32) * s, 'bk': jax.random.normal(ks[4], (EMB,), dtype=jnp.float32) * 0.01, 'wv': jax.random.normal(ks[5], (EMB, EMB), dtype=jnp.float32) * s, 'bv': jax.random.normal(ks[6], (EMB,), dtype=jnp.float32) * 0.01, 'wo': jax.random.normal(ks[7], (EMB, EMB), dtype=jnp.float32) * s, 'bo': jax.random.normal(ks[8], (EMB,), dtype=jnp.float32) * 0.01}
        return inp
    _L1_conv_all = _L1_conv_setup()
    _L1_conv_in = {k: v for k, v in _L1_conv_all.items() if k in ('gn_gamma', 'gn_beta', 'wq', 'bq', 'wk', 'bk', 'wv', 'bv', 'wo', 'bo')}
    del _L1_conv_all

    def _L2_conv_setup():
        import jax, jax.numpy as jnp
        import numpy as np
        C = 256
        NUM_HEADS = 8
        GROUPS = min(32, C // 4)
        EPS = 1e-05
        SCALE = (C // NUM_HEADS) ** (-0.5)

        def _group_norm(x, gamma, beta):
            B, Cc, H, W = x.shape
            xg = x.reshape(B, GROUPS, Cc // GROUPS, H, W)
            mean = jnp.mean(xg, axis=(2, 3, 4), keepdims=True)
            var = jnp.var(xg, axis=(2, 3, 4), keepdims=True)
            xg = (xg - mean) * jax.lax.rsqrt(var + EPS)
            x = xg.reshape(B, Cc, H, W)
            return x * gamma[None, :, None, None] + beta[None, :, None, None]
        key = jax.random.key(seed)
        ks = jax.random.split(key, 7)
        B, H, W = (8, 32, 32)
        x = jax.random.normal(ks[0], (B, C, H, W), dtype=jnp.float32)
        gamma = jnp.ones((C,), dtype=jnp.float32)
        beta = jnp.zeros((C,), dtype=jnp.float32)
        w_qkv = jax.random.normal(ks[1], (3 * C, C), dtype=jnp.float32) * C ** (-0.5)
        b_qkv = jax.random.normal(ks[2], (3 * C,), dtype=jnp.float32) * 0.01
        w_proj = jax.random.normal(ks[3], (C, C), dtype=jnp.float32) * C ** (-0.5)
        b_proj = jax.random.normal(ks[4], (C,), dtype=jnp.float32) * 0.01
        return {'x': x, 'gamma': gamma, 'beta': beta, 'w_qkv': w_qkv, 'b_qkv': b_qkv, 'w_proj': w_proj, 'b_proj': b_proj}
    _L2_conv_all = _L2_conv_setup()
    _L2_conv_in = {k: v for k, v in _L2_conv_all.items() if k in ('gamma', 'beta', 'w_qkv', 'b_qkv', 'w_proj', 'b_proj')}
    del _L2_conv_all

    def _L3_conv_setup():
        import jax, jax.numpy as jnp
        import numpy as np
        C_IN = 256
        OUT_CH = 128
        DIM = 32
        key = jax.random.key(seed)
        ks = jax.random.split(key, 11)
        b, c, h, w = (16, C_IN, 32, 32)

        def winit(k, o, i):
            s = 1.0 / np.sqrt(i)
            return jax.random.uniform(k, (o, i), jnp.float32, -s, s)
        return {'x': jax.random.normal(ks[0], (b, c, h, w), jnp.float32), 'Wq': winit(ks[1], OUT_CH, C_IN), 'bq': winit(ks[2], OUT_CH, C_IN)[:, 0], 'Wk': winit(ks[3], OUT_CH, C_IN), 'bk': winit(ks[4], OUT_CH, C_IN)[:, 0], 'Wv': winit(ks[5], C_IN, C_IN), 'bv': winit(ks[6], C_IN, C_IN)[:, 0], 'Ws': winit(ks[7], DIM, C_IN), 'bs': winit(ks[8], DIM, C_IN)[:, 0], 'We': winit(ks[9], DIM, C_IN), 'be': winit(ks[10], DIM, C_IN)[:, 0]}
    _L3_conv_all = _L3_conv_setup()
    _L3_conv_in = {k: v for k, v in _L3_conv_all.items() if k in ('Wq', 'bq', 'Wk', 'bk', 'Wv', 'bv', 'Ws', 'bs', 'We', 'be')}
    del _L3_conv_all
    return {'x': x, 'L0_conv_w_qkv': _L0_conv_in['w_qkv'], 'L0_conv_w_proj': _L0_conv_in['w_proj'], 'L0_conv_b_proj': _L0_conv_in['b_proj'], 'L0_conv_pos_bias': _L0_conv_in['pos_bias'], 'L0_conv_gamma': _L0_conv_in['gamma'], 'L0_conv_beta': _L0_conv_in['beta'], 'L1_conv_gn_gamma': _L1_conv_in['gn_gamma'], 'L1_conv_gn_beta': _L1_conv_in['gn_beta'], 'L1_conv_wq': _L1_conv_in['wq'], 'L1_conv_bq': _L1_conv_in['bq'], 'L1_conv_wk': _L1_conv_in['wk'], 'L1_conv_bk': _L1_conv_in['bk'], 'L1_conv_wv': _L1_conv_in['wv'], 'L1_conv_bv': _L1_conv_in['bv'], 'L1_conv_wo': _L1_conv_in['wo'], 'L1_conv_bo': _L1_conv_in['bo'], 'L2_conv_gamma': _L2_conv_in['gamma'], 'L2_conv_beta': _L2_conv_in['beta'], 'L2_conv_w_qkv': _L2_conv_in['w_qkv'], 'L2_conv_b_qkv': _L2_conv_in['b_qkv'], 'L2_conv_w_proj': _L2_conv_in['w_proj'], 'L2_conv_b_proj': _L2_conv_in['b_proj'], 'L3_conv_Wq': _L3_conv_in['Wq'], 'L3_conv_bq': _L3_conv_in['bq'], 'L3_conv_Wk': _L3_conv_in['Wk'], 'L3_conv_bk': _L3_conv_in['bk'], 'L3_conv_Wv': _L3_conv_in['Wv'], 'L3_conv_bv': _L3_conv_in['bv'], 'L3_conv_Ws': _L3_conv_in['Ws'], 'L3_conv_bs': _L3_conv_in['bs'], 'L3_conv_We': _L3_conv_in['We'], 'L3_conv_be': _L3_conv_in['be']}

def reference(x, L0_conv_w_qkv, L0_conv_w_proj, L0_conv_b_proj, L0_conv_pos_bias, L0_conv_gamma, L0_conv_beta, L1_conv_gn_gamma, L1_conv_gn_beta, L1_conv_wq, L1_conv_bq, L1_conv_wk, L1_conv_bk, L1_conv_wv, L1_conv_bv, L1_conv_wo, L1_conv_bo, L2_conv_gamma, L2_conv_beta, L2_conv_w_qkv, L2_conv_b_qkv, L2_conv_w_proj, L2_conv_b_proj, L3_conv_Wq, L3_conv_bq, L3_conv_Wk, L3_conv_bk, L3_conv_Wv, L3_conv_bv, L3_conv_Ws, L3_conv_bs, L3_conv_We, L3_conv_be):
    import jax
    import jax.numpy as jnp

    def _L0_conv_ref(x, w_qkv, w_proj, b_proj, pos_bias, gamma, beta):
        import jax, jax.numpy as jnp
        import numpy as np
        CH = 256
        HEADS = 8
        REDUCTION = 2
        INNER = max(CH // REDUCTION, HEADS)
        POS_RES = 16
        LN_EPS = 1e-05
        B, C, H, W = x.shape
        d_head = INNER // HEADS
        scale = jnp.float32(d_head ** (-0.5))
        qkv = jnp.einsum('oc,bchw->bohw', w_qkv, x)
        q, k, v = jnp.split(qkv, 3, axis=1)

        def heads_view(t):
            return t.reshape(B, HEADS, d_head, H * W)
        q, k, v = (heads_view(q), heads_view(k), heads_view(v))
        attn = jnp.einsum('bhdi,bhdj->bhij', q * scale, k)
        pos = jax.image.resize(pos_bias, (1, HEADS, H, W), method='bilinear')
        pos = pos.reshape(1, HEADS, H * W)
        attn = attn + pos[..., :, None] + pos[..., None, :]
        attn = jax.nn.softmax(attn, axis=-1)
        y = jnp.einsum('bhij,bhdj->bhdi', attn, v)
        y = y.reshape(B, INNER, H, W)
        y = jnp.einsum('co,bohw->bchw', w_proj, y) + b_proj[None, :, None, None]
        z = (x + y).transpose(0, 2, 3, 1)
        mu = jnp.mean(z, axis=-1, keepdims=True)
        var = jnp.var(z, axis=-1, keepdims=True)
        z = (z - mu) / jnp.sqrt(var + LN_EPS) * gamma + beta
        return z.transpose(0, 3, 1, 2)

    def _L1_conv_ref(input, gn_gamma, gn_beta, wq, bq, wk, bk, wv, bv, wo, bo):
        import jax, jax.numpy as jnp
        import numpy as np
        import math
        HEADS = 8
        DIM_HEAD = 32
        EMB = 256
        GROUPS = 32
        EPS = 100000.0
        B, D, H, W = input.shape
        S = H * W
        residual = input
        xg = input.reshape(B, GROUPS, D // GROUPS * H * W)
        mu = jnp.mean(xg, axis=-1, keepdims=True)
        var = jnp.var(xg, axis=-1, keepdims=True)
        xn = (xg - mu) / jnp.sqrt(var + EPS)
        xn = xn.reshape(B, D, H, W) * gn_gamma[:, None, None] + gn_beta[:, None, None]
        x = xn.reshape(B, D, S).transpose(0, 2, 1)
        q = (x @ wq.T + bq).reshape(B, S, HEADS, DIM_HEAD).transpose(0, 2, 1, 3)
        k = (x @ wk.T + bk).reshape(B, S, HEADS, DIM_HEAD).transpose(0, 2, 1, 3)
        v = (x @ wv.T + bv).reshape(B, S, HEADS, DIM_HEAD).transpose(0, 2, 1, 3)
        scale = 1.0 / math.sqrt(DIM_HEAD)
        scores = jnp.einsum('bhqd,bhkd->bhqk', q * scale, k)
        attn = jax.nn.softmax(scores, axis=-1)
        o = jnp.einsum('bhqk,bhkd->bhqd', attn, v)
        o = o.transpose(0, 2, 1, 3).reshape(B, S, D)
        out = o @ wo.T + bo
        out = out.transpose(0, 2, 1).reshape(B, D, H, W)
        return out + residual

    def _L2_conv_ref(x, gamma, beta, w_qkv, b_qkv, w_proj, b_proj):
        import jax, jax.numpy as jnp
        import numpy as np
        C = 256
        NUM_HEADS = 8
        GROUPS = min(32, C // 4)
        EPS = 1e-05
        SCALE = (C // NUM_HEADS) ** (-0.5)

        def _group_norm(x, gamma, beta):
            B, Cc, H, W = x.shape
            xg = x.reshape(B, GROUPS, Cc // GROUPS, H, W)
            mean = jnp.mean(xg, axis=(2, 3, 4), keepdims=True)
            var = jnp.var(xg, axis=(2, 3, 4), keepdims=True)
            xg = (xg - mean) * jax.lax.rsqrt(var + EPS)
            x = xg.reshape(B, Cc, H, W)
            return x * gamma[None, :, None, None] + beta[None, :, None, None]
        B, Cc, H, W = x.shape
        nh, hd = (NUM_HEADS, Cc // NUM_HEADS)
        HW = H * W
        h = _group_norm(x, gamma, beta)
        qkv = jnp.einsum('oc,bchw->bohw', w_qkv, h) + b_qkv[None, :, None, None]
        qkv = qkv.reshape(B, 3, nh, hd, HW)
        q, k, v = (qkv[:, 0], qkv[:, 1], qkv[:, 2])
        scores = jnp.einsum('bhcq,bhck->bhqk', q, k) * SCALE
        attn = jax.nn.softmax(scores, axis=-1)
        out = jnp.einsum('bhqk,bhck->bhcq', attn, v)
        out = out.reshape(B, Cc, H, W)
        out = jnp.einsum('oc,bchw->bohw', w_proj, out) + b_proj[None, :, None, None]
        return x + out

    def _L3_conv_ref(x, Wq, bq, Wk, bk, Wv, bv, Ws, bs, We, be):
        import jax, jax.numpy as jnp
        import numpy as np
        C_IN = 256
        OUT_CH = 128
        DIM = 32
        b, c, h, w = x.shape
        n = h * w
        xf = x.reshape(b, c, n)
        Q = jnp.einsum('oc,bcn->bon', Wq, xf) + bq[:, None]
        K = jnp.einsum('oc,bcn->bon', Wk, xf) + bk[:, None]
        gate = jax.nn.sigmoid(jnp.mean(Q * K, axis=1, keepdims=True))
        V = jnp.einsum('oc,bcn->bon', Wv, xf) + bv[:, None]
        V_dw = V * gate
        Qs = jnp.einsum('oc,bcn->bon', Ws, xf) + bs[:, None]
        Ke = jnp.einsum('oc,bcn->bon', We, xf) + be[:, None]
        energy = jnp.einsum('bcn,bdn->bcd', V_dw, Qs)
        attention = jax.nn.softmax(energy, axis=-1)
        Vout = jnp.einsum('bcd,bdn->bcn', attention, Ke)
        return x + Vout.reshape(b, c, h, w)

    def _gn(v, G=32, eps=1e-05):
        B_, C_, H_, W_ = v.shape
        g = v.reshape(B_, G, C_ // G, H_, W_)
        m = jnp.mean(g, axis=(2, 3, 4), keepdims=True)
        s = jnp.var(g, axis=(2, 3, 4), keepdims=True)
        return ((g - m) / jnp.sqrt(s + eps)).reshape(v.shape)

    def _ln_c(v, eps=1e-06):
        m = jnp.mean(v, axis=1, keepdims=True)
        s = jnp.var(v, axis=1, keepdims=True)
        return (v - m) / jnp.sqrt(s + eps)

    def _ln_t(v, eps=1e-05):
        m = jnp.mean(v, axis=-1, keepdims=True)
        s = jnp.var(v, axis=-1, keepdims=True)
        return (v - m) / jnp.sqrt(s + eps)

    def _to_tokens(v):
        B_, C_, H_, W_ = v.shape
        return v.reshape(B_, C_, H_ * W_).transpose(0, 2, 1)

    def _from_tokens(t, like):
        B_, C_, H_, W_ = like.shape
        return t.transpose(0, 2, 1).reshape(B_, C_, H_, W_)
    x = _L0_conv_ref(x, L0_conv_w_qkv, L0_conv_w_proj, L0_conv_b_proj, L0_conv_pos_bias, L0_conv_gamma, L0_conv_beta)
    x = _L1_conv_ref(x, L1_conv_gn_gamma, L1_conv_gn_beta, L1_conv_wq, L1_conv_bq, L1_conv_wk, L1_conv_bk, L1_conv_wv, L1_conv_bv, L1_conv_wo, L1_conv_bo)
    x = _L2_conv_ref(x, L2_conv_gamma, L2_conv_beta, L2_conv_w_qkv, L2_conv_b_qkv, L2_conv_w_proj, L2_conv_b_proj)
    x = _L3_conv_ref(x, L3_conv_Wq, L3_conv_bq, L3_conv_Wk, L3_conv_bk, L3_conv_Wv, L3_conv_bv, L3_conv_Ws, L3_conv_bs, L3_conv_We, L3_conv_be)
    return x

_drawn_inputs = setup_inputs


def setup_inputs(seed=0):
    import zlib

    import numpy as np

    out = dict(_drawn_inputs(seed))
    spreads = {'L0_conv_b_proj': (0.0, 0.1),
     'L0_conv_gamma': (1.0, 0.2),
     'L0_conv_beta': (0.0, 0.1),
     'L1_conv_gn_gamma': (1.0, 0.6),
     'L1_conv_gn_beta': (0.0, 0.1),
     'L2_conv_gamma': (1.0, 0.2),
     'L2_conv_beta': (0.0, 0.1)}
    factors = {'L0_conv_w_qkv': 4.852,
     'L0_conv_w_proj': 5.553,
     'L0_conv_pos_bias': 8.0,
     'L1_conv_wq': 200.0,
     'L1_conv_bq': 200.0,
     'L1_conv_wk': 200.0,
     'L1_conv_bk': 200.0,
     'L3_conv_Wq': 5.666,
     'L3_conv_bq': 8.0,
     'L3_conv_Wk': 5.355,
     'L3_conv_bk': 8.0}
    for name, (base, spread) in spreads.items():
        noise = np.random.default_rng([zlib.crc32(name.encode()), seed]).standard_normal(out[name].shape)
        drawn = base * np.exp(spread * noise) if base else spread * noise
        out[name] = jnp.asarray(drawn.astype(out[name].dtype))
    for name, factor in factors.items():
        out[name] = (out[name] * factor).astype(out[name].dtype)
    return out
```

```python
from contextlib import ExitStack

import concourse.bass as bass
from concourse import mybir

F32 = mybir.dt.float32
F32R = mybir.dt.float32r
ALU = mybir.AluOpType
ACT = mybir.ActivationFunctionType
AX = mybir.AxisListType

P = 128
C = 256
KC = C // P
N = 1024
HALF = 512
NH = 8
TILES = N // P
DP = 32
SPLIT_ROWS = 3 * DP
SHIFT_ROWS = SPLIT_ROWS + 2
LEAD = 12
LAG = 2
STEPS = NH * TILES
E_BUFS = 4
LAYERS = 3
HEAD_DIM = (16, 32, 32)
NORM_GROUP = 8
EPS_LN = 1e-5
EPS_GN = (None, 1e5, 1e-5)
L3_COLS = 128 + 128 + 256 + 32
L3_DIM = 32
RES = 16
W_COLS = (3 * 128 + C, 4 * C, 4 * C)


def attention_chain(nc, x, w0, w1, w2, w3, pos_bias, cols, row3, out):
    ctx = ExitStack()
    with ctx:
        def sb(name, shape, dt=F32):
            return ctx.enter_context(nc.sbuf_tensor(name, shape, dt))

        def sem(name):
            return ctx.enter_context(nc.semaphore(name))

        X = sb("X", [P, KC, N])
        XN = sb("XN", [P, KC, N])
        q_full = sb("q_full", [P, 4, HALF])
        qH = sb("qH", [P, 2, N], F32R)
        qL = sb("qL", [P, 2, N], F32R)
        kH = sb("kH", [P, 2, N], F32R)
        kL = sb("kL", [P, 2, N], F32R)
        q_stack = sb("q_stack", [P, NH, N], F32R)
        k_stack = sb("k_stack", [P, NH, N], F32R)
        V = sb("V", [P, TILES, NH * DP])
        E = sb("E", [P, E_BUFS, N])
        ones = sb("ones", [P, P])
        att = sb("att", [P, KC, N])
        pv_sb = sb("pv_sb", [P, HALF])
        den_sb = sb("den_sb", [P, HALF])
        rec_sb = sb("rec_sb", [P, HALF])
        W = [sb(f"W{l}", [P, KC, W_COLS[l]]) for l in range(LAYERS)]
        W3 = sb("W3", [P, KC, L3_COLS + L3_DIM])
        col = sb("col", [P, 40])
        max16 = sb("max16", [P, 2, 2 * TILES])
        negmax = sb("negmax", [P, 2, TILES])
        mH = sb("mH", [TILES, 2, P], F32R)
        mL = sb("mL", [TILES, 2, P], F32R)
        ident = sb("ident", [P, P])
        group_avg = sb("group_avg", [P, P])
        chan_avg = sb("chan_avg", [P, P])
        stats = sb("stats", [P, KC, 2, 6])
        mv = sb("mv", [P, KC, 2])
        gsmall = sb("gsmall", [P, 8, KC])
        qbias = sb("qbias", [P, 2])
        obias = sb("obias", [P, KC])
        eps = sb("eps", [P, 3])
        posH = sb("posH", [NH, N], F32R)
        posL = sb("posL", [NH, N], F32R)
        bias3 = sb("bias3", [P, L3_COLS])
        gate = sb("gate", [P, 4, TILES])
        energy = sb("energy", [P, 3, KC, L3_DIM])
        esum = sb("esum", [P, 3, KC])
        pos_v = E[0:NH, 1, 0:HALF].rearrange("p (y x) -> p y x", x=RES)
        pos_t = E[0:NH, 1, HALF:N].rearrange("p (y x) -> p y x", x=RES)
        one_rows = E[0:NH, 2, :]
        pos_in = E[0:NH, 3, 0:RES * RES].rearrange("p (y x) -> p y x", x=RES)
        Ke = att[0:L3_DIM, 0, :]
        attT = att[0:L3_DIM, 1, 0:C]
        pos = att[0:NH, 0, :]
        QKV3 = E[:, :, :].rearrange("p a (b n) -> p (a b) n", n=HALF)
        QS3 = V[:, :, 0:L3_DIM]
        QK3 = V[:, :, P:2 * P]

        B = ctx.enter_context(nc.psum_tensor("B", [P, 4, HALF], F32))
        A = ctx.enter_context(nc.psum_tensor("A", [P, 2, HALF], F32))
        PV = ctx.enter_context(nc.psum_tensor("PV", [P, HALF], F32))
        M = ctx.enter_context(nc.psum_tensor("M", [P, HALF], F32))

        B_PROJ, GAM, BET = [(0, 1), (12, 13), (24, 25)], [(2, 3), (14, 15), (26, 27)], [(4, 5), (16, 17), (28, 29)]
        BQ, BK, BV = [None, (6, 7), (18, 19)], [None, (8, 9), (20, 21)], [None, (10, 11), (22, 23)]
        BE = 30

        x_in, cols_in, w_in, pos_dma, row_in, out_dma = (sem("x_in"), sem("cols_in"), [sem(f"w_in{l}") for l in range(4)],
                                                         sem("pos_dma"), sem("row_in"), sem("out_dma"))
        const_set, stacks_zero, ones_rows_set, v_zero = sem("const_set"), sem("stacks_zero"), sem("ones_rows_set"), sem("v_zero")
        pool_chain, dve_chain, act_chain = sem("pool_chain"), sem("dve_chain"), sem("act_chain")
        pos_ready, pos_rows = sem("pos_ready"), sem("pos_rows")
        xn_ready = sem("xn_ready")
        qbias_set = sem("qbias_set")
        proj_done, proj_used = sem("proj_done"), sem("proj_used")
        full_ready = sem("full_ready")
        split_ready = sem("split_ready")
        stack_dma = [sem(f"stack_dma{h}") for h in range(NH)]
        stack_free = sem("stack_free")
        a_done, a_used = sem("a_done"), sem("a_used")
        negmax_ready, rows_done, rows_used = sem("negmax_ready"), sem("rows_done"), sem("rows_used")
        shift_dma = [sem(f"shift_dma{i}") for i in range(2)]
        b_done, e_ready, pv_done, pv_used = sem("b_done"), sem("e_ready"), sem("pv_done"), sem("pv_used")
        rec_ready, att_ready = sem("rec_ready"), sem("att_ready")
        out_done, x_ready = sem("out_done"), sem("x_ready")
        stat_ready, stat_done = sem("stat_ready"), sem("stat_done")
        sd_ready = sem("sd_ready")
        vb_done = sem("vb_done")
        ln_in, ln_done, sq_ready = sem("ln_in"), sem("ln_done"), sem("sq_ready")
        t_done, t_used, qs_ready, en_done, gate_sums, max_ready = sem("t_done"), sem("t_used"), sem("qs_ready"), sem("en_done"), sem("gate_sums"), sem("max_ready")
        attn3, at_done, at_used, ke_done, ke_used, vo_done, fin_ready = (sem("attn3"), sem("at_done"), sem("at_used"),
            sem("ke_done"), sem("ke_used"), sem("vo_done"), sem("fin_ready"))

        UNITS = [[("q", 0, 0), ("q", 0, 1), ("k", 0, 0), ("k", 0, 1), ("v", 0, 4), ("v", 4, 4)]]
        for _ in range(2):
            UNITS.append([("q", 0, 0), ("q", 0, 1), ("k", 0, 0), ("k", 0, 1)] + [("v", t, 2) for t in (0, 2, 4, 6)]
                         + [("q", 1, 0), ("q", 1, 1), ("k", 1, 0), ("k", 1, 1)])
        UNIT0 = [sum(len(u) for u in UNITS[:l]) for l in range(LAYERS)]
        QK0 = [sum(sum(x[0] != "v" for x in u) for u in UNITS[:l]) for l in range(LAYERS)]

        def qk_index(l, n):
            return QK0[l] + sum(x[0] != "v" for x in UNITS[l][:n])

        LATE = [{}, {0: 8, 2: 9, 4: 10, 6: 11}, {0: 8, 2: 9, 4: 10, 6: 11}]
        HEAD_ROWS = (16, 32, 32)
        STACK_DMAS = 6

        def stack_count(l):
            return 16 * STACK_DMAS * (l + 1)

        block = ctx.enter_context(nc.Block())

        def head_source(l, h):
            return (0, 16 * h) if l == 0 else (h // 4, DP * (h % 4))

        def load_stack(eng, l, h):
            c, p = head_source(l, h)
            rows = HEAD_ROWS[l]
            for dst, src, blk in ((q_stack, qH, 0), (k_stack, kH, 0), (q_stack, qH, 1), (k_stack, kL, 1),
                                  (q_stack, qL, 2), (k_stack, kH, 2)):
                eng.dma_start(dst[DP * blk:DP * blk + rows, h, :].bitcast(F32),
                              src[p:p + rows, c, :].bitcast(F32)).then_inc(stack_dma[h], 16)

        @block.sync
        def _(sp):
            for c in range(KC):
                sp.dma_start(X[:, c, :], x[c]).then_inc(x_in, 16)
                if c == 0:
                    sp.dma_start(W[0][:, :, :], w0).then_inc(w_in[0], 16)
            sp.dma_start(W[1][:, :, :], w1).then_inc(w_in[1], 16)
            sp.dma_start(W[2][:, :, :], w2).then_inc(w_in[2], 16)
            sp.dma_start(W3[:, :, :], w3).then_inc(w_in[3], 16)
            sp.dma_start(bias3[:, :], row3.to_broadcast([P, L3_COLS])).then_inc(row_in, 16)
            sp.wait_ge(stacks_zero, 2)
            sp.wait_ge(pos_ready, 3)
            for dst, r, src in ((q_stack, 16, posH[:, :].bitcast(F32)), (q_stack, 17, posL[:, :].bitcast(F32)),
                                (k_stack, 18, posH[:, :].bitcast(F32)), (k_stack, 19, posL[:, :].bitcast(F32)),
                                (k_stack, 16, one_rows[:, :]), (k_stack, 17, one_rows[:, :]),
                                (q_stack, 18, one_rows[:, :]), (q_stack, 19, one_rows[:, :])):
                sp.dma_start(dst[r:r + 1, :, :].bitcast(F32), src).then_inc(pos_rows, 16)

            def shift_rows(l, h):
                n = l * NH + h
                sp.wait_ge(rows_used, 2 * (n + 1))
                for r, src in ((0, mH), (1, mL)):
                    sp.dma_start(q_stack[SPLIT_ROWS + r:SPLIT_ROWS + r + 1, h, :].bitcast(F32)
                                 .rearrange("o (t c) -> o t c", t=TILES),
                                 src[:, n % 2, :].bitcast(F32)).then_inc(shift_dma[n % 2], 16)

            for l in range(LAYERS):
                sp.wait_ge(split_ready, QK0[l] + 4)
                if l == 1:
                    sp.wait_ge(pos_rows, 16 * 8)
                sp.wait_ge(b_done, STEPS * l) if l else None
                for h in range(NH if l == 0 else 4):
                    load_stack(sp, l, h)
                shift_rows(l, 0)
                if l:
                    sp.wait_ge(split_ready, QK0[l] + 8)
                    for h in range(4, 6):
                        load_stack(sp, l, h)
                shift_rows(l, 1)
                if l:
                    for h in range(6, NH):
                        load_stack(sp, l, h)
                for h in range(2, NH):
                    shift_rows(l, h)
            for n in range(4):
                sp.wait_ge(fin_ready, n + 1)
                sp.dma_start(out[n // 2, :, HALF * (n % 2):HALF * (n % 2 + 1)],
                             XN[:, n // 2, HALF * (n % 2):HALF * (n % 2 + 1)]).then_inc(out_dma, 16)
            sp.wait_ge(out_dma, 64)

        @block.gpsimd
        def _(pool):
            pool.memset(ident[:, :], 0.0).then_inc(pool_chain, 1)
            pool.memset(group_avg[:, :], 1.0 / NORM_GROUP).then_inc(pool_chain, 1)
            pool.memset(chan_avg[:, :], 1.0 / C).then_inc(const_set, 1)
            pool.memset(ones[:, :], 1.0).then_inc(const_set, 1)
            pool.memset(one_rows[:, :], 1.0).then_inc(pos_ready, 1)
            pool.memset(eps[:, 0:1], EPS_LN).then_inc(const_set, 1)
            pool.memset(eps[:, 1:2], EPS_GN[1]).then_inc(const_set, 1)
            pool.memset(eps[:, 2:3], EPS_GN[2]).then_inc(const_set, 1)
            pool.wait_ge(pool_chain, 2)
            pool.affine_select(out=ident[:, :], in_=ident[:, :], compare_op=ALU.not_equal, fill=1.0, base=0,
                               pattern=[[-1, P]], channel_multiplier=1).then_inc(const_set, 1)
            ga = group_avg[:, :].rearrange("p (g j) -> p g j", j=NORM_GROUP)
            pool.affine_select(out=ga, in_=ga, compare_op=ALU.is_ge, fill=0.0, base=0,
                               pattern=[[-NORM_GROUP, P // NORM_GROUP], [0, NORM_GROUP]],
                               channel_multiplier=1).then_inc(pool_chain, 1)
            pool.wait_ge(pool_chain, 3)
            pool.affine_select(out=ga, in_=ga, compare_op=ALU.is_ge, fill=0.0, base=NORM_GROUP - 1,
                               pattern=[[NORM_GROUP, P // NORM_GROUP], [0, NORM_GROUP]],
                               channel_multiplier=-1).then_inc(const_set, 1)
            for l in range(LAYERS):
                for h in range(NH):
                    n = l * NH + h
                    r = 64 * (h % 2)
                    if h % 2 == 0:
                        pool.wait_ge(rec_ready, n // 2 + 1)
                    if h == 0 and l:
                        pool.wait_ge(out_done, 4 * l)
                    for half in range(2):
                        src = slice(r + DP * half, r + DP * half + DP)
                        pool.tensor_tensor(att[DP * (h % 4):DP * (h % 4) + DP, h // 4, HALF * half:HALF * (half + 1)],
                                           pv_sb[src, :], rec_sb[src, :], ALU.mult).then_inc(att_ready, 1)

        @block.scalar
        def _(act):
            act.dma_start(col[:, :], cols).then_inc(cols_in, 16)
            act.dma_start(pos_in[:, :, :], pos_bias[0]).then_inc(pos_dma, 16)
            chain = [0]

            def link(ins):
                chain[0] += 1
                ins.then_inc(act_chain, 1)
                act.wait_ge(act_chain, chain[0])

            def project_out(l, n):
                kind, c, half = UNITS[l][n]
                u = UNIT0[l] + n
                act.wait_ge(proj_done, u + 1)
                if kind == "v":
                    t, tiles = c, half
                    if l == 0:
                        act.activation(V[:, t:t + tiles, :].rearrange("p t (h d) -> p t h d", d=DP)[:, :, :, 0:16],
                                       B[:, u % 4, :].rearrange("p (t h d) -> p t h d", t=tiles, d=16),
                                       ACT.Copy).then_inc(proj_used, 1)
                    else:
                        act.activation(V[:, t:t + tiles, :], B[:, u % 4, :].rearrange("p (t d) -> p t d", t=tiles),
                                       ACT.Copy).then_inc(proj_used, 1)
                    return
                i = qk_index(l, n)
                high = (qH if kind == "q" else kH)[:, c, HALF * half:HALF * (half + 1)]
                scale = float(HEAD_DIM[l]) ** -0.5 if kind == "q" else 1.0
                bias = 0.0
                if l:
                    bias = qbias[:, c:c + 1] if kind == "q" else col[:, BK[l][c]:BK[l][c] + 1]
                if i >= 4:
                    act.wait_ge(split_ready, i - 3)
                act.activation(q_full[:, i % 4, :], B[:, u % 4, :], ACT.Identity, bias=bias,
                               scale=scale).then_inc(full_ready, 1)
                act.activation(high, B[:, u % 4, :], ACT.Identity, bias=bias, scale=scale).then_inc(proj_used, 1)

            def probabilities(l, s):
                g = l * STEPS + s
                act.wait_ge(b_done, g + 1)
                if g >= E_BUFS:
                    act.wait_ge(pv_done, g + 1 - E_BUFS)
                act.activation(E[:, g % E_BUFS, :], B[:, 2 * (g % 2):2 * (g % 2) + 2, :].rearrange("p a b -> p (a b)"),
                               ACT.Exp).then_inc(e_ready, 1)

            def pv_out(l, h):
                n = l * NH + h
                r = 64 * (h % 2)
                act.wait_ge(pv_done, TILES * (n + 1))
                if n >= 2:
                    act.wait_ge(rec_ready, n // 2)
                    act.wait_ge(att_ready, 2 * (n - 1) if h % 2 else 2 * n)
                act.activation(den_sb[r:r + 64, :], PV[64:128, :], ACT.Copy).then_inc(pv_used, 1)
                act.activation(pv_sb[r:r + 64, :], PV[0:64, :], ACT.Copy).then_inc(pv_used, 1)

            for l in range(LAYERS):
                if l == 1:
                    for i in range(2):
                        act.wait_ge(ln_in, 2 * i + 2)
                        act.activation(XN[:, i, :], att[:, i, :], ACT.Square).then_inc(sq_ready, 1)
                    act.wait_ge(ln_done, 3)
                    act.wait_ge(const_set, 7)
                    act.activation(E[:, 0, :], B[:, 0:2, :].rearrange("p a b -> p (a b)"), ACT.Sqrt,
                                   bias=eps[:, 0:1]).then_inc(sd_ready, 1)
                if l:
                    act.wait_ge(stat_done, 2 * l)
                    act.activation(gsmall[:, 4, :], M[:, 4:6], ACT.Sqrt,
                                   bias=eps[:, l:l + 1]).then_inc(sd_ready, 1)
                    act.wait_ge(qbias_set, l)
                for n in range(len(UNITS[l])):
                    if l == 0 and n == 4:
                        act.wait_ge(v_zero, 1)
                    project_out(l, n)
                for s in range(STEPS):
                    probabilities(l, s)
                    if s % TILES == LAG - 1 and s > TILES:
                        pv_out(l, s // TILES - 1)
                pv_out(l, NH - 1)
            act.wait_ge(row_in, 16)
            for c in range(2):
                act.wait_ge(ke_done, c + 1)
                act.activation(Ke[:, HALF * c:HALF * (c + 1)], B[0:L3_DIM, 2 + c, :], ACT.Identity,
                               bias=col[0:L3_DIM, BE:BE + 1]).then_inc(ke_used, 1)
            act.wait_ge(gate_sums, TILES)
            act.activation(gate[:, 1, :], gate[:, 0, :], ACT.Exp, scale=-1.0 / 128).then_inc(sd_ready, 1)
            act.wait_ge(max_ready, 1)
            for c in range(KC):
                act.activation(energy[:, 0, c, :], M[:, L3_DIM * c:L3_DIM * (c + 1)], ACT.Exp,
                               bias=esum[:, 0, c:c + 1], accum_out=esum[:, 1, c:c + 1]).then_inc(sd_ready, 1)

        @block.vector
        def _(dve):
            chain = [0]

            def link(ins):
                chain[0] += 1
                ins.then_inc(dve_chain, 1)
                dve.wait_ge(dve_chain, chain[0])

            dve.memset(q_stack[0:SPLIT_ROWS, :, :].bitcast(F32), 0.0).then_inc(stacks_zero, 1)
            dve.memset(k_stack[0:SPLIT_ROWS, :, :].bitcast(F32), 0.0).then_inc(stacks_zero, 1)
            dve.memset(k_stack[SPLIT_ROWS:P, :, :].bitcast(F32), 1.0).then_inc(ones_rows_set, 1)
            dve.memset(V[:, :, :], 0.0).then_inc(v_zero, 1)
            dve.wait_ge(pos_dma, 16)
            pv_rows = pos_v[:, :, :].rearrange("p (y two) x -> p y two x", two=2)
            tmp_rows = pos_t[:, :, :].rearrange("p (y two) x -> p y two x", two=2)
            link(dve.tensor_scalar(pos_t[:, 0:RES, :], pos_in[:, :, :], 0.25, None, ALU.mult))
            link(dve.tensor_scalar(pos_t[:, RES:2 * RES, :], pos_in[:, :, :], 0.75, None, ALU.mult))
            quarter, most = pos_t[:, 0:RES, :], pos_t[:, RES:2 * RES, :]
            link(dve.tensor_tensor(pv_rows[:, 1:RES, 0, :], most[:, 1:RES, :], quarter[:, 0:RES - 1, :], ALU.add))
            link(dve.tensor_tensor(pv_rows[:, 0:RES - 1, 1, :], most[:, 0:RES - 1, :], quarter[:, 1:RES, :], ALU.add))
            link(dve.tensor_copy(pv_rows[:, 0, 0, :], pos_in[:, 0, :]))
            link(dve.tensor_copy(pv_rows[:, RES - 1, 1, :], pos_in[:, RES - 1, :]))
            pos_x = pos.rearrange("p (y x two) -> p y x two", y=2 * RES, two=2)
            link(dve.tensor_scalar(pos_t[:, :, :], pos_v[:, :, :], 0.25, None, ALU.mult))
            link(dve.scalar_tensor_tensor(out=pos_x[:, :, 1:RES, 0], in0=pos_v[:, :, 1:RES], scalar=0.75,
                                          in1=pos_t[:, :, 0:RES - 1], op0=ALU.mult, op1=ALU.add))
            link(dve.scalar_tensor_tensor(out=pos_x[:, :, 0:RES - 1, 1], in0=pos_v[:, :, 0:RES - 1], scalar=0.75,
                                          in1=pos_t[:, :, 1:RES], op0=ALU.mult, op1=ALU.add))
            link(dve.tensor_copy(pos_x[:, :, 0, 0], pos_v[:, :, 0]))
            link(dve.tensor_copy(pos_x[:, :, RES - 1, 1], pos_v[:, :, RES - 1]))
            dve.tensor_copy(posH[:, :], pos).then_inc(pos_ready, 1)
            dve.wait_ge(pos_ready, 2)
            dve.tensor_tensor(posL[:, :], pos, posH[:, :].bitcast(F32), ALU.subtract).then_inc(pos_ready, 1)
            dve.wait_ge(cols_in, 16)

            def split(l, n):
                kind, c, half = UNITS[l][n]
                i = qk_index(l, n)
                cols_ = slice(HALF * half, HALF * (half + 1))
                dve.wait_ge(proj_used, UNIT0[l] + n + 1)
                dve.tensor_tensor((qL if kind == "q" else kL)[:, c, cols_], q_full[:, i % 4, :],
                                  (qH if kind == "q" else kH)[:, c, cols_].bitcast(F32),
                                  ALU.subtract).then_inc(split_ready, 1)

            def maxima(l, a):
                n = l * NH + a // TILES
                for half in range(2):
                    u = 2 * (l * STEPS + a) + half
                    dve.wait_ge(a_done, u + 1)
                    if a % TILES == 0 and half == 0 and n >= 2:
                        dve.wait_ge(negmax_ready, n - 1)
                    dve.tensor_reduce(max16[:, n % 2, half * TILES + a % TILES:half * TILES + a % TILES + 1],
                                      A[:, u % 2, :], AX.X, ALU.max, negate=True).then_inc(a_used, 1)
                if a % TILES == TILES - 1:
                    dve.wait_ge(a_used, 2 * (l * STEPS + a + 1))
                    if n >= 2:
                        dve.wait_ge(rows_done, n - 1)
                    dve.tensor_tensor(negmax[:, n % 2, :], max16[:, n % 2, 0:TILES],
                                      max16[:, n % 2, TILES:2 * TILES], ALU.min).then_inc(negmax_ready, 1)

            def max_rows(l, h):
                n = l * NH + h
                dve.wait_ge(rows_done, n + 1)
                if n >= 2:
                    dve.wait_ge(shift_dma[n % 2], 32 * (n // 2))
                dve.tensor_copy(mH[:, n % 2, :], M[0:TILES, 0:P]).then_inc(rows_used, 1)
                dve.wait_ge(rows_used, 2 * n + 1)
                dve.tensor_tensor(mL[:, n % 2, :], M[0:TILES, 0:P], mH[:, n % 2, :].bitcast(F32),
                                  ALU.subtract).then_inc(rows_used, 1)

            def reciprocals(l, pair):
                n = l * NH // 2 + pair
                dve.wait_ge(pv_used, 4 * (n + 1))
                if n:
                    dve.wait_ge(att_ready, 4 * n)
                dve.reciprocal(rec_sb[:, :], den_sb[:, :]).then_inc(rec_ready, 1)

            def group_norm(l):
                g = gsmall
                for c in range(KC):
                    link(dve.bn_aggr(mv[:, c, :], stats[:, c, :, :].rearrange("p a b -> p (a b)")))
                dve.tensor_copy(g[:, 0, :], mv[:, :, 0]).then_inc(stat_ready, 1)
                dve.wait_ge(stat_ready, 2 * l - 1)
                dve.wait_ge(stat_done, 2 * l - 1)
                link(dve.tensor_copy(g[:, 7, :], M[:, 2:4]))
                link(dve.tensor_tensor(g[:, 1, :], g[:, 0, :], g[:, 7, :], ALU.subtract))
                link(dve.tensor_tensor(g[:, 2, :], g[:, 1, :], g[:, 1, :], ALU.mult))
                dve.tensor_tensor(g[:, 3, :], g[:, 2, :], mv[:, :, 1], ALU.add).then_inc(stat_ready, 1)
                dve.wait_ge(sd_ready, l + 1)
                link(dve.reciprocal(g[:, 5, :], g[:, 4, :]))
                link(dve.tensor_tensor(g[:, 5, :], g[:, 5, :], col[:, GAM[l][0]:GAM[l][1] + 1], ALU.mult))
                link(dve.tensor_tensor(g[:, 6, :], g[:, 7, :], g[:, 5, :], ALU.mult))
                link(dve.tensor_tensor(g[:, 6, :], col[:, BET[l][0]:BET[l][1] + 1], g[:, 6, :], ALU.subtract))
                for c in range(KC):
                    dve.tensor_scalar(XN[:, c, :], X[:, c, :], g[:, 5, c:c + 1], g[:, 6, c:c + 1],
                                      ALU.mult, ALU.add).then_inc(xn_ready, 1)
                dve.tensor_scalar(qbias[:, :], col[:, BQ[l][0]:BQ[l][1] + 1], float(HEAD_DIM[l]) ** -0.5, None,
                                  ALU.mult).then_inc(qbias_set, 1)

            def block_stats():
                for c in range(KC):
                    for half in range(2):
                        link(dve.bn_stats(stats[:, c, half, :], X[:, c, HALF * half:HALF * (half + 1)]))

            for l in range(LAYERS):
                if l:
                    group_norm(l)
                n_units = len(UNITS[l])
                late = set(LATE[l].values())
                for n in range(n_units):
                    if UNITS[l][n][0] != "v" and n not in late:
                        split(l, n)
                for a in range(LEAD):
                    maxima(l, a)
                    if a in LATE[l]:
                        split(l, LATE[l][a])
                    if a == TILES - 1:
                        max_rows(l, 0)
                for s in range(STEPS):
                    a = s + LEAD
                    if s % TILES == TILES - 3 and s // TILES + 1 < NH:
                        max_rows(l, s // TILES + 1)
                    if a < STEPS:
                        maxima(l, a)
                    if s % (2 * TILES) == LAG + 1 and s > 2 * TILES:
                        reciprocals(l, s // (2 * TILES) - 1)
                reciprocals(l, NH // 2 - 1)
                if l == 0:
                    link(dve.tensor_copy(obias[:, :], col[:, B_PROJ[0][0]:B_PROJ[0][1] + 1]))
                else:
                    dve.wait_ge(vb_done, l)
                    link(dve.tensor_tensor(obias[:, :], M[:, 0:2], col[:, B_PROJ[l][0]:B_PROJ[l][1] + 1], ALU.add))
                for u in range(4):
                    c, half = u // 2, u % 2
                    cs = slice(HALF * half, HALF * (half + 1))
                    dve.wait_ge(out_done, 4 * l + u + 1)
                    dve.scalar_tensor_tensor(out=X[:, c, cs], in0=B[:, u, :], scalar=obias[:, c:c + 1],
                                             in1=X[:, c, cs], op0=ALU.add, op1=ALU.add).then_inc(x_ready, 1)
                dve.wait_ge(x_ready, 4 * (l + 1))
                if l == 0:
                    dve.wait_ge(ln_done, 1)
                    for c in range(KC):
                        for half in range(2):
                            cs = slice(HALF * half, HALF * (half + 1))
                            dve.tensor_tensor(att[:, c, cs], X[:, c, cs], A[:, half, :], ALU.subtract).then_inc(ln_in, 1)
                    dve.wait_ge(ln_in, 4)
                    dve.wait_ge(sd_ready, 1)
                    for half in range(2):
                        cs = slice(HALF * half, HALF * (half + 1))
                        link(dve.reciprocal(E[:, 1, cs], E[:, 0, cs]))
                    for c in range(KC):
                        link(dve.tensor_tensor(att[:, c, :], att[:, c, :], E[:, 1, :], ALU.mult))
                        link(dve.tensor_scalar(X[:, c, :], att[:, c, :], col[:, GAM[0][c]:GAM[0][c] + 1],
                                               col[:, BET[0][c]:BET[0][c] + 1], ALU.mult, ALU.add))
                if l < 2:
                    block_stats()
            dve.wait_ge(row_in, 16)
            for t in range(TILES):
                b = t % 2
                dve.wait_ge(t_done, t + 1)
                dve.tensor_tensor(QKV3[:, t, :], B[:, b, :], bias3[:, 0:HALF], ALU.add).then_inc(dve_chain, 1)
                chain[0] += 1
                dve.tensor_tensor(QS3[:, t, :], A[:, b, 0:L3_DIM], bias3[:, HALF:L3_COLS],
                                  ALU.add).then_inc(t_used, 1)
                dve.wait_ge(dve_chain, chain[0])
                link(dve.tensor_tensor(QK3[:, t, :], QKV3[:, t, 0:P], QKV3[:, t, P:2 * P], ALU.mult))
                dve.tensor_reduce(gate[:, 0, t:t + 1], QK3[:, t, :], AX.X, ALU.add).then_inc(gate_sums, 1)
            dve.wait_ge(sd_ready, 4)
            link(dve.tensor_scalar(gate[:, 2, :], gate[:, 1, :], 1.0, None, ALU.add))
            link(dve.reciprocal(gate[:, 3, :], gate[:, 2, :]))
            for t in range(TILES):
                dve.tensor_scalar(QS3[:, t, :], QS3[:, t, :], gate[:, 3, t:t + 1], None,
                                  ALU.mult).then_inc(qs_ready, 1)
            dve.wait_ge(en_done, 1)
            dve.tensor_reduce(esum[:, 0, :], M[:, 0:KC * L3_DIM].rearrange("p (c d) -> p c d", c=KC), AX.X, ALU.max,
                              negate=True).then_inc(max_ready, 1)
            dve.wait_ge(sd_ready, 6)
            link(dve.reciprocal(esum[:, 2, :], esum[:, 1, :]))
            for c in range(KC):
                dve.tensor_scalar(energy[:, 1, c, :], energy[:, 0, c, :], esum[:, 2, c:c + 1], None,
                                  ALU.mult).then_inc(attn3, 1)
            dve.wait_ge(at_done, 1)
            dve.tensor_copy(attT[:, :], M[0:L3_DIM, 0:C]).then_inc(at_used, 1)
            for u in range(4):
                c, half = u // 2, u % 2
                cs = slice(HALF * half, HALF * (half + 1))
                dve.wait_ge(vo_done, u + 1)
                dve.tensor_tensor(XN[:, c, cs], B[:, u, :], X[:, c, cs], ALU.add).then_inc(fin_ready, 1)

        @block.tensor
        def _(pe):
            def projection(l, n):
                kind, c, half = UNITS[l][n]
                u = UNIT0[l] + n
                src = X if l == 0 else XN
                if n >= 4:
                    pe.wait_ge(proj_used, u - 3)
                if kind == "v":
                    t, tiles = c, half
                    wide = HALF // tiles
                    for j in range(tiles):
                        for kc in range(KC):
                            mm = pe.matmul(B[:, u % 4, wide * j:wide * (j + 1)],
                                           src[:, kc, P * (t + j):P * (t + j + 1)],
                                           W[l][:, kc, 2 * wide:3 * wide], start=(kc == 0), stop=(kc == KC - 1))
                else:
                    wide = P if l == 0 else C
                    off = (0 if kind == "q" else wide) + P * c
                    for kc in range(KC):
                        mm = pe.matmul(B[:, u % 4, :], W[l][:, kc, off:off + P],
                                       src[:, kc, HALF * half:HALF * (half + 1)],
                                       start=(kc == 0), stop=(kc == KC - 1))
                mm.then_inc(proj_done, 1)

            def scores_for_max(l, a):
                h, t = a // TILES, a % TILES
                if t == 0:
                    pe.wait_ge(stack_dma[h], stack_count(l))
                for half in range(2):
                    u = 2 * (l * STEPS + a) + half
                    if u >= 2:
                        pe.wait_ge(a_used, u - 1)
                    pe.matmul(A[:, u % 2, :], q_stack[0:SPLIT_ROWS, h, P * t:P * (t + 1)],
                              k_stack[0:SPLIT_ROWS, h, HALF * half:HALF * (half + 1)],
                              start=True, stop=True).then_inc(a_done, 1)

            def transpose_max(l, h):
                n = l * NH + h
                pe.wait_ge(negmax_ready, n + 1)
                if n:
                    pe.wait_ge(rows_used, 2 * n)
                pe.transpose(M[0:TILES, 0:P], negmax[:, n % 2, :], ident[:, :]).then_inc(rows_done, 1)

            def scores(l, s):
                g = l * STEPS + s
                h, t = s // TILES, s % TILES
                if t == 0:
                    n = l * NH + h
                    pe.wait_ge(shift_dma[n % 2], 32 * (n // 2 + 1))
                if g >= 2:
                    pe.wait_ge(e_ready, g - 1)
                for half in range(2):
                    mm = pe.matmul(B[:, 2 * (g % 2) + half, :], k_stack[0:SHIFT_ROWS, h, P * t:P * (t + 1)],
                                   q_stack[0:SHIFT_ROWS, h, HALF * half:HALF * (half + 1)],
                                   start=True, stop=True)
                mm.then_inc(b_done, 1)

            def values(l, s):
                g = l * STEPS + s
                h, t = s // TILES, s % TILES
                n = l * NH + h
                pe.wait_ge(e_ready, g + 1)
                if t == 0 and n:
                    pe.wait_ge(pv_used, 2 * n)
                for part, lhs in enumerate((V[:, t, DP * h:DP * (h + 1)], ones[:, 0:DP])):
                    for half in range(2):
                        r = 64 * part + DP * half
                        mm = pe.matmul(PV[r:r + DP, :], lhs, E[:, g % E_BUFS, HALF * half:HALF * (half + 1)],
                                       start=(t == 0), stop=(t == TILES - 1))
                mm.then_inc(pv_done, 1)

            pe.wait_ge(const_set, 7)
            for l in range(LAYERS):
                pe.wait_ge(w_in[l], 16)
                if l == 0:
                    pe.wait_ge(x_in, 16 * KC)
                else:
                    pe.wait_ge(stat_ready, 2 * l - 1)
                    pe.matmul(M[:, 2:4], group_avg[:, :], gsmall[:, 0, :], start=True, stop=True).then_inc(stat_done, 1)
                    pe.wait_ge(stat_ready, 2 * l)
                    pe.matmul(M[:, 4:6], group_avg[:, :], gsmall[:, 3, :], start=True, stop=True).then_inc(stat_done, 1)
                    pe.wait_ge(xn_ready, 2 * l)
                late = set(LATE[l].values())
                for n in range(len(UNITS[l])):
                    if n not in late:
                        projection(l, n)
                if l == 0:
                    pe.wait_ge(ones_rows_set, 1)
                    pe.wait_ge(pos_rows, 16 * 8)
                for a in range(LEAD):
                    scores_for_max(l, a)
                    if a in LATE[l]:
                        projection(l, LATE[l][a])
                    if a == TILES - 1:
                        transpose_max(l, 0)
                pe.wait_ge(proj_used, UNIT0[l] + len(UNITS[l]))
                for s in range(STEPS):
                    scores(l, s)
                    if s % TILES == TILES - 3 and s // TILES + 1 < NH:
                        transpose_max(l, s // TILES + 1)
                    if s + LEAD < STEPS:
                        scores_for_max(l, s + LEAD)
                    if s >= LAG:
                        values(l, s - LAG)
                for s in range(STEPS - LAG, STEPS):
                    values(l, s)
                wo = (W_COLS[l] - C)
                if l:
                    for c in range(KC):
                        for kc in range(KC):
                            mm = pe.matmul(M[:, c:c + 1], W[l][:, kc, wo + P * c:wo + P * (c + 1)],
                                           col[:, BV[l][kc]:BV[l][kc] + 1], start=(kc == 0), stop=(kc == KC - 1))
                    mm.then_inc(vb_done, 1)
                pe.wait_ge(e_ready, STEPS * (l + 1))
                for kc in range(KC):
                    pe.wait_ge(att_ready, 2 * (l * NH + 4 * (kc + 1)))
                    for u in range(4):
                        c, half = u // 2, u % 2
                        mm = pe.matmul(B[:, u, :], W[l][:, kc, wo + P * c:wo + P * (c + 1)],
                                       att[:, kc, HALF * half:HALF * (half + 1)], start=(kc == 0), stop=(kc == KC - 1))
                        if kc == KC - 1:
                            mm.then_inc(out_done, 1)
                if l == 0:
                    pe.wait_ge(x_ready, 4)
                    for half in range(2):
                        for kc in range(KC):
                            mm = pe.matmul(A[:, half, :], chan_avg[:, :], X[:, kc, HALF * half:HALF * (half + 1)],
                                           start=(kc == 0), stop=(kc == KC - 1))
                    mm.then_inc(ln_done, 1)
                    pe.wait_ge(sq_ready, 2)
                    for half in range(2):
                        for kc in range(KC):
                            mm = pe.matmul(B[:, half, :], chan_avg[:, :], XN[:, kc, HALF * half:HALF * (half + 1)],
                                           start=(kc == 0), stop=(kc == KC - 1))
                        mm.then_inc(ln_done, 1)
            pe.wait_ge(w_in[3], 16)
            pe.wait_ge(x_ready, 4 * LAYERS)
            for c in range(2):
                for kc in range(KC):
                    mm = pe.matmul(B[0:L3_DIM, 2 + c, :], W3[:, kc, L3_COLS:L3_COLS + L3_DIM],
                                   X[:, kc, HALF * c:HALF * (c + 1)], start=(kc == 0), stop=(kc == KC - 1))
                mm.then_inc(ke_done, 1)
            for t in range(TILES):
                b = t % 2
                if t >= 2:
                    pe.wait_ge(t_used, t - 1)
                for kc in range(KC):
                    pe.matmul(B[:, b, :], X[:, kc, P * t:P * (t + 1)], W3[:, kc, 0:HALF],
                              start=(kc == 0), stop=(kc == KC - 1))
                for kc in range(KC):
                    mm = pe.matmul(A[:, b, 0:L3_DIM], X[:, kc, P * t:P * (t + 1)], W3[:, kc, HALF:L3_COLS],
                                   start=(kc == 0), stop=(kc == KC - 1))
                mm.then_inc(t_done, 1)
            for c in range(KC):
                for t in range(TILES):
                    if c == 0:
                        pe.wait_ge(qs_ready, t + 1)
                    mm = pe.matmul(M[:, L3_DIM * c:L3_DIM * (c + 1)], QKV3[:, t, 256 + P * c:256 + P * (c + 1)],
                                   QS3[:, t, :], start=(t == 0), stop=(t == TILES - 1))
            mm.then_inc(en_done, 1)
            for c in range(KC):
                pe.wait_ge(attn3, c + 1)
                mm = pe.transpose(M[0:L3_DIM, P * c:P * (c + 1)], energy[:, 1, c, :], ident[:, :])
            mm.then_inc(at_done, 1)
            pe.wait_ge(at_used, 1)
            pe.wait_ge(ke_used, 2)
            for u in range(4):
                c, half = u // 2, u % 2
                pe.matmul(B[:, u, :], attT[:, P * c:P * (c + 1)], Ke[:, HALF * half:HALF * (half + 1)],
                          start=True, stop=True).then_inc(vo_done, 1)


def kernel(**inputs):
    import numpy as np
    from concourse import bacc
    from concourse.bass_utils import run_bass_kernel_spmd

    g = {k: np.ascontiguousarray(v) for k, v in inputs.items()}

    def chunks(w):
        return np.ascontiguousarray(w.reshape(KC, P, -1).transpose(1, 0, 2))

    wp0 = np.zeros((NH, DP, C), np.float32)
    wp0[:, 0:16] = g["L0_conv_w_proj"].T.reshape(NH, 16, C)
    w0 = chunks(np.concatenate([g["L0_conv_w_qkv"].T, wp0.reshape(NH * DP, C)], 1))
    w1 = chunks(np.concatenate([g[f"L1_conv_w{n}"].T for n in "qkvo"], 1))
    w2 = chunks(np.concatenate([g["L2_conv_w_qkv"].T, g["L2_conv_w_proj"].T], 1))
    w3 = chunks(np.concatenate([g[f"L3_conv_W{n}"].T for n in "qkvse"], 1))
    vectors = [g["L0_conv_b_proj"], g["L0_conv_gamma"], g["L0_conv_beta"],
               g["L1_conv_bq"], g["L1_conv_bk"], g["L1_conv_bv"],
               g["L1_conv_bo"], g["L1_conv_gn_gamma"], g["L1_conv_gn_beta"],
               g["L2_conv_b_qkv"][0:C], g["L2_conv_b_qkv"][C:2 * C], g["L2_conv_b_qkv"][2 * C:],
               g["L2_conv_b_proj"], g["L2_conv_gamma"], g["L2_conv_beta"]]
    cols = np.zeros((P, 40), np.float32)
    for i, v in enumerate(vectors):
        cols[:, 2 * i:2 * i + 2] = v.reshape(KC, P).T
    cols[0:L3_DIM, 30] = g["L3_conv_be"]
    row3 = np.concatenate([g[f"L3_conv_b{n}"] for n in "qkvs"])[None, :]
    arrays = {"x_in_dram": g["x"].reshape(KC, P, N), "w0_dram": w0, "w1_dram": w1, "w2_dram": w2, "w3_dram": w3,
              "pos_dram": g["L0_conv_pos_bias"], "cols_dram": cols, "row3_dram": row3}
    nc = bacc.Bacc("TRN2", target_bir_lowering=False, num_devices=1)
    args = [nc.dram_tensor(n, a.shape, mybir.dt.from_np(a.dtype), kind="ExternalInput").ap() for n, a in arrays.items()]
    out = nc.dram_tensor("out_dram", (KC, P, N), F32, kind="ExternalOutput").ap()
    attention_chain(nc, *args, out)
    r = run_bass_kernel_spmd(nc, [arrays], core_ids=[0])
    return r.results[0]["out_dram"].reshape(1, C, 32, 32)
```

```python
from contextlib import ExitStack

import concourse.bass as bass
from concourse import mybir

F32 = mybir.dt.float32
F32R = mybir.dt.float32r
ALU = mybir.AluOpType
ACT = mybir.ActivationFunctionType
AX = mybir.AxisListType

P = 128
C = 256
KC = C // P
N = 1024
HALF = 512
NH = 8
TILES = N // P
DP = 32
LEAD = 12
LAG = 2
STEPS = NH * TILES
E_BUFS = 4
LAYERS = 3
HEAD_DIM = (16, 32, 32)
POS_ROWS = 4
SPLIT_ROWS = tuple(3 * d + (POS_ROWS if d == 16 else 0) for d in HEAD_DIM)
SHIFT_ROWS = tuple(n + 2 for n in SPLIT_ROWS)
REC_PARTS = 8
NORM_GROUP = 8
EPS_LN = 1e-5
EPS_GN = (None, 1e5, 1e-5)
L3_COLS = 128 + 128 + 256 + 32
L3_DIM = 32
RES = 16
W_COLS = (3 * 128 + C, 4 * C, 4 * C)


def attention_chain(nc, x, w0, w1, w2, w3, pos_bias, cols, row3, out):
    ctx = ExitStack()
    with ctx:
        def sb(name, shape, dt=F32):
            return ctx.enter_context(nc.sbuf_tensor(name, shape, dt))

        def sem(name):
            return ctx.enter_context(nc.semaphore(name))

        X = sb("X", [P, KC, N])
        XN = sb("XN", [P, KC, N])
        q_full = sb("q_full", [P, 4, HALF])
        qH = sb("qH", [P, 2, N], F32R)
        qL = sb("qL", [P, 2, N], F32R)
        kH = sb("kH", [P, 2, N], F32R)
        kL = sb("kL", [P, 2, N], F32R)
        q_stack = sb("q_stack", [P, NH, N], F32R)
        k_stack = sb("k_stack", [P, NH, N], F32R)
        V = sb("V", [P, TILES, NH * DP])
        E = sb("E", [P, E_BUFS, N])
        ones = sb("ones", [P, P])
        att = sb("att", [P, KC, N])
        pv_sb = sb("pv_sb", [P, 2, HALF])
        den_sb = sb("den_sb", [P, 2, HALF])
        rec_sb = sb("rec_sb", [P, HALF])
        W = [sb(f"W{l}", [P, KC, W_COLS[l]]) for l in range(LAYERS)]
        W3 = sb("W3", [P, KC, L3_COLS + L3_DIM])
        col = sb("col", [P, 40])
        max16 = sb("max16", [P, 2, 2 * TILES])
        negmax = sb("negmax", [P, 2, TILES])
        mH = sb("mH", [TILES, 2, P], F32R)
        mL = sb("mL", [TILES, 2, P], F32R)
        ident = sb("ident", [P, P])
        group_avg = sb("group_avg", [P, P])
        chan_avg = sb("chan_avg", [P, P])
        stats = sb("stats", [P, KC, 2, 6])
        rstd8 = sb("rstd8", [P, 2, TILES])
        spare = sb("spare", [P, 2])
        mv = sb("mv", [P, KC, 2])
        gsmall = sb("gsmall", [P, 8, KC])
        qbias = sb("qbias", [P, 2])
        obias = sb("obias", [P, KC])
        eps = sb("eps", [P, 3])
        posH = sb("posH", [NH, N], F32R)
        posL = sb("posL", [NH, N], F32R)
        bias3 = sb("bias3", [P, L3_COLS])
        gate = sb("gate", [P, 4, TILES])
        energy = sb("energy", [P, 3, KC, L3_DIM])
        esum = sb("esum", [P, 3, KC])
        pos_v = E[0:NH, 1, 0:HALF].rearrange("p (y x) -> p y x", x=RES)
        pos_t = E[0:NH, 1, HALF:N].rearrange("p (y x) -> p y x", x=RES)
        one_rows = E[0:NH, 2, :]
        pos_in = E[0:NH, 3, 0:RES * RES].rearrange("p (y x) -> p y x", x=RES)
        Ke = att[0:L3_DIM, 0, :]
        attT = att[0:L3_DIM, 1, 0:C]
        pos = att[0:NH, 0, :]
        QKV3 = E[:, :, :].rearrange("p a (b n) -> p (a b) n", n=HALF)
        QS3 = V[:, :, 0:L3_DIM]
        QK3 = V[:, :, P:2 * P]

        B = ctx.enter_context(nc.psum_tensor("B", [P, 4, HALF], F32))
        A = ctx.enter_context(nc.psum_tensor("A", [P, 2, HALF], F32))
        PV = ctx.enter_context(nc.psum_tensor("PV", [P, HALF], F32))
        M = ctx.enter_context(nc.psum_tensor("M", [P, HALF], F32))

        B_PROJ, GAM, BET = [(0, 1), (12, 13), (24, 25)], [(2, 3), (14, 15), (26, 27)], [(4, 5), (16, 17), (28, 29)]
        BQ, BK, BV = [None, (6, 7), (18, 19)], [None, (8, 9), (20, 21)], [None, (10, 11), (22, 23)]
        BE = 30

        x_in, cols_in, w_in, pos_dma, row_in, out_dma = (sem("x_in"), sem("cols_in"), [sem(f"w_in{l}") for l in range(4)],
                                                         sem("pos_dma"), sem("row_in"), sem("out_dma"))
        const_set, v_zero = sem("const_set"), sem("v_zero")
        pool_chain, dve_chain, act_chain = sem("pool_chain"), sem("dve_chain"), sem("act_chain")
        pos_ready, pos_rows = sem("pos_ready"), sem("pos_rows")
        xn_ready = sem("xn_ready")
        qbias_set = sem("qbias_set")
        proj_done, proj_used = sem("proj_done"), sem("proj_used")
        full_ready = sem("full_ready")
        split_ready = sem("split_ready")
        stack_dma = [sem(f"stack_dma{h}") for h in range(NH)]
        a_done, a_used = sem("a_done"), sem("a_used")
        negmax_ready, rows_done, rows_used = sem("negmax_ready"), sem("rows_done"), sem("rows_used")
        shift_dma = [sem(f"shift_dma{i}") for i in range(2)]
        b_done, e_ready, pv_done, pv_used = sem("b_done"), sem("e_ready"), sem("pv_done"), sem("pv_used")
        rec_ready, att_ready, att_tail = sem("rec_ready"), sem("att_ready"), sem("att_tail")
        out_done, x_ready = sem("out_done"), sem("x_ready")
        stats_in, stat_ready, stat_done = sem("stats_in"), sem("stat_ready"), sem("stat_done")
        sd_ready = sem("sd_ready")
        vb_done = sem("vb_done")
        ln_in, ln_done, sq_ready = sem("ln_in"), sem("ln_done"), sem("sq_ready")
        rstd_ready, ln_scaled, ln_out, eps_read = sem("rstd_ready"), sem("ln_scaled"), sem("ln_out"), sem("eps_read")
        t_done, t_used, qs_ready, en_done, gate_sums, max_ready = sem("t_done"), sem("t_used"), sem("qs_ready"), sem("en_done"), sem("gate_sums"), sem("max_ready")
        attn3, at_done, at_used, ke_done, ke_used, vo_done, fin_ready = (sem("attn3"), sem("at_done"), sem("at_used"),
            sem("ke_done"), sem("ke_used"), sem("vo_done"), sem("fin_ready"))

        UNITS = [[("q", 0, 0), ("q", 0, 1), ("k", 0, 0), ("k", 0, 1), ("v", 0, 4), ("v", 4, 4)]]
        for _ in range(2):
            UNITS.append([("q", 0, 0), ("q", 0, 1), ("k", 0, 0), ("k", 0, 1)] + [("v", t, 2) for t in (0, 2, 4, 6)]
                         + [("q", 1, 0), ("q", 1, 1), ("k", 1, 0), ("k", 1, 1)])
        UNIT0 = [sum(len(u) for u in UNITS[:l]) for l in range(LAYERS)]
        QK0 = [sum(sum(x[0] != "v" for x in u) for u in UNITS[:l]) for l in range(LAYERS)]

        def qk_index(l, n):
            return QK0[l] + sum(x[0] != "v" for x in UNITS[l][:n])

        LATE = [{}, {0: 8, 2: 9, 4: 10, 6: 11}, {0: 8, 2: 9, 4: 10, 6: 11}]
        STACK_DMAS = 6

        def stack_count(l):
            return 16 * STACK_DMAS * (l + 1)

        REC_LAYER = 3 * REC_PARTS + 3

        def rec_count(l, h):
            return l * REC_LAYER + (REC_PARTS * (h // 2 + 1) if h < 6 else 3 * REC_PARTS + (1 if h == 6 else 3))

        UNIT_ORDER = (0, 2, 1, 3)
        QUARTER = HALF // 2

        block = ctx.enter_context(nc.Block())

        def head_source(l, h):
            return (0, 16 * h) if l == 0 else (h // 4, DP * (h % 4))

        def load_stack(eng, l, h):
            c, p = head_source(l, h)
            rows = HEAD_DIM[l]
            for dst, src, blk in ((q_stack, qH, 0), (k_stack, kH, 0), (q_stack, qH, 1), (k_stack, kL, 1),
                                  (q_stack, qL, 2), (k_stack, kH, 2)):
                eng.dma_start(dst[rows * blk:rows * (blk + 1), h, :].bitcast(F32),
                              src[p:p + rows, c, :].bitcast(F32)).then_inc(stack_dma[h], 16)

        @block.sync
        def _(sp):
            for c in range(KC):
                sp.dma_start(X[:, c, :], x[c]).then_inc(x_in, 16)
                if c == 0:
                    sp.dma_start(W[0][:, :, :], w0).then_inc(w_in[0], 16)
            sp.dma_start(W[1][:, :, :], w1).then_inc(w_in[1], 16)
            sp.dma_start(W[2][:, :, :], w2).then_inc(w_in[2], 16)
            sp.dma_start(W3[:, :, :], w3).then_inc(w_in[3], 16)
            sp.dma_start(bias3[:, :], row3.to_broadcast([P, L3_COLS])).then_inc(row_in, 16)
            sp.wait_ge(pos_ready, 3)
            p0 = SPLIT_ROWS[0] - POS_ROWS
            highs, lows = posH[:, :].bitcast(F32), posL[:, :].bitcast(F32)
            for dst, r, src in ((q_stack, p0, highs), (q_stack, p0 + 1, lows), (k_stack, p0 + 2, highs),
                                (k_stack, p0 + 3, lows), (k_stack, p0, one_rows), (k_stack, p0 + 1, one_rows),
                                (q_stack, p0 + 2, one_rows), (q_stack, p0 + 3, one_rows),
                                (k_stack, p0 + 4, one_rows), (k_stack, p0 + 5, one_rows),
                                (k_stack, SPLIT_ROWS[1], one_rows), (k_stack, SPLIT_ROWS[1] + 1, one_rows)):
                sp.dma_start(dst[r:r + 1, :, :].bitcast(F32), src).then_inc(pos_rows, 16)

            def shift_rows(l, h):
                n = l * NH + h
                sp.wait_ge(rows_used, 2 * (n + 1))
                for r, src in ((0, mH), (1, mL)):
                    sp.dma_start(q_stack[SPLIT_ROWS[l] + r:SPLIT_ROWS[l] + r + 1, h, :].bitcast(F32)
                                 .rearrange("o (t c) -> o t c", t=TILES),
                                 src[:, n % 2, :].bitcast(F32)).then_inc(shift_dma[n % 2], 16)

            for l in range(LAYERS):
                sp.wait_ge(split_ready, QK0[l] + 4)
                if l:
                    sp.wait_ge(b_done, STEPS * l)
                for h in range(2):
                    load_stack(sp, l, h)
                for h in range(NH):
                    if h + 2 == 4 and l:
                        sp.wait_ge(split_ready, QK0[l] + 8)
                    if h + 2 < NH:
                        load_stack(sp, l, h + 2)
                    shift_rows(l, h)
            for n in range(4):
                sp.wait_ge(fin_ready, n + 1)
                sp.dma_start(out[n // 2, :, HALF * (n % 2):HALF * (n % 2 + 1)],
                             XN[:, n // 2, HALF * (n % 2):HALF * (n % 2 + 1)]).then_inc(out_dma, 16)
            sp.wait_ge(out_dma, 64)

        @block.gpsimd
        def _(pool):
            pool.memset(ident[:, :], 0.0).then_inc(pool_chain, 1)
            pool.memset(group_avg[:, :], 1.0 / NORM_GROUP).then_inc(pool_chain, 1)
            pool.memset(chan_avg[:, :], 1.0 / C).then_inc(const_set, 1)
            pool.memset(ones[:, :], 1.0).then_inc(const_set, 1)
            pool.memset(one_rows[:, :], 1.0).then_inc(pos_ready, 1)
            pool.memset(eps[:, 0:1], EPS_LN).then_inc(const_set, 1)
            pool.memset(eps[:, 1:2], EPS_GN[1]).then_inc(const_set, 1)
            pool.memset(eps[:, 2:3], EPS_GN[2]).then_inc(const_set, 1)
            pool.wait_ge(pool_chain, 2)
            pool.affine_select(out=ident[:, :], in_=ident[:, :], compare_op=ALU.not_equal, fill=1.0, base=0,
                               pattern=[[-1, P]], channel_multiplier=1).then_inc(const_set, 1)
            ga = group_avg[:, :].rearrange("p (g j) -> p g j", j=NORM_GROUP)
            pool.affine_select(out=ga, in_=ga, compare_op=ALU.is_ge, fill=0.0, base=0,
                               pattern=[[-NORM_GROUP, P // NORM_GROUP], [0, NORM_GROUP]],
                               channel_multiplier=1).then_inc(pool_chain, 1)
            pool.wait_ge(pool_chain, 3)
            pool.affine_select(out=ga, in_=ga, compare_op=ALU.is_ge, fill=0.0, base=NORM_GROUP - 1,
                               pattern=[[NORM_GROUP, P // NORM_GROUP], [0, NORM_GROUP]],
                               channel_multiplier=-1).then_inc(const_set, 1)
            pool.memset(V[:, :, :], 0.0).then_inc(v_zero, 1)
            for l in range(LAYERS):
                for h in range(NH):
                    n = l * NH + h
                    r = 64 * (h % 2)
                    last = h == NH - 1
                    if last:
                        pool.wait_ge(rec_ready, rec_count(l, h) - 1)
                    else:
                        pool.wait_ge(rec_ready, rec_count(l, h))
                    if h == 0 and l:
                        pool.wait_ge(out_done, 4 * l)
                    wide = QUARTER if last else HALF
                    for half in range(2):
                        src = slice(r + DP * half, r + DP * half + DP)
                        pool.tensor_tensor(att[DP * (h % 4):DP * (h % 4) + DP, h // 4, HALF * half:HALF * half + wide],
                                           pv_sb[src, h // 2 % 2, 0:wide], rec_sb[src, 0:wide], ALU.mult).then_inc(att_ready, 1)

        @block.scalar
        def _(act):
            act.dma_start(col[:, :], cols).then_inc(cols_in, 16)
            act.dma_start(pos_in[:, :, :], pos_bias[0]).then_inc(pos_dma, 16)
            chain = [0]

            def link(ins):
                chain[0] += 1
                ins.then_inc(act_chain, 1)
                act.wait_ge(act_chain, chain[0])

            def project_out(l, n):
                kind, c, half = UNITS[l][n]
                u = UNIT0[l] + n
                act.wait_ge(proj_done, u + 1)
                if kind == "v":
                    t, tiles = c, half
                    if l == 0:
                        act.activation(V[:, t:t + tiles, :].rearrange("p t (h d) -> p t h d", d=DP)[:, :, :, 0:16],
                                       B[:, u % 4, :].rearrange("p (t h d) -> p t h d", t=tiles, d=16),
                                       ACT.Copy).then_inc(proj_used, 1)
                    else:
                        act.activation(V[:, t:t + tiles, :], B[:, u % 4, :].rearrange("p (t d) -> p t d", t=tiles),
                                       ACT.Copy).then_inc(proj_used, 1)
                    return
                i = qk_index(l, n)
                high = (qH if kind == "q" else kH)[:, c, HALF * half:HALF * (half + 1)]
                scale = float(HEAD_DIM[l]) ** -0.5 if kind == "q" else 1.0
                bias = 0.0
                if l:
                    bias = qbias[:, c:c + 1] if kind == "q" else col[:, BK[l][c]:BK[l][c] + 1]
                if i >= 4:
                    act.wait_ge(split_ready, i - 3)
                act.activation(q_full[:, i % 4, :], B[:, u % 4, :], ACT.Identity, bias=bias,
                               scale=scale).then_inc(full_ready, 1)
                act.activation(high, B[:, u % 4, :], ACT.Identity, bias=bias, scale=scale).then_inc(proj_used, 1)

            def probabilities(l, s):
                g = l * STEPS + s
                act.wait_ge(b_done, g + 1)
                if g >= E_BUFS:
                    act.wait_ge(pv_done, g + 1 - E_BUFS)
                act.activation(E[:, g % E_BUFS, :], B[:, 2 * (g % 2):2 * (g % 2) + 2, :].rearrange("p a b -> p (a b)"),
                               ACT.Exp).then_inc(e_ready, 1)

            def pv_out(l, h):
                n = l * NH + h
                r = 64 * (h % 2)
                act.wait_ge(pv_done, TILES * (n + 1))
                if n >= 4:
                    before = (l, h - 4) if h >= 4 else (l - 1, h + NH - 4)
                    act.wait_ge(rec_ready, rec_count(*before))
                    act.wait_ge(att_ready, 2 * (n - 3))
                if l and h == 3:
                    act.wait_ge(att_tail, 2 * l)
                slot = h // 2 % 2
                act.activation(den_sb[r:r + 64, slot, :], PV[64:128, :], ACT.Copy).then_inc(pv_used, 1)
                act.activation(pv_sb[r:r + 64, slot, :], PV[0:64, :], ACT.Copy).then_inc(pv_used, 1)

            for l in range(LAYERS):
                if l == 1:
                    for i, u in enumerate(UNIT_ORDER):
                        cs = slice(HALF * (u % 2), HALF * (u % 2 + 1))
                        act.wait_ge(ln_in, i + 1)
                        act.activation(XN[:, u // 2, cs], att[:, u // 2, cs], ACT.Square).then_inc(sq_ready, 1)
                    act.wait_ge(ln_done, 3)
                    act.activation(rstd8[:, 0, :], M[:, 8:8 + TILES], ACT.Sqrt, bias=eps[:, 0:1]).then_inc(sd_ready, 1)
                    for i, u in enumerate(UNIT_ORDER):
                        c, cs = u // 2, slice(HALF * (u % 2), HALF * (u % 2 + 1))
                        act.wait_ge(ln_scaled, i + 1)
                        act.activation(X[:, c, cs], X[:, c, cs], ACT.Identity, scale=col[:, GAM[0][c]:GAM[0][c] + 1],
                                       bias=col[:, BET[0][c]:BET[0][c] + 1]).then_inc(ln_out, 1)
                if l:
                    act.wait_ge(stat_done, 2 * l)
                    act.activation(gsmall[:, 4, :], M[:, 4:6], ACT.Sqrt,
                                   bias=eps[:, l:l + 1]).then_inc(sd_ready, 1)
                    act.activation(spare[:, 1:2], eps[:, 0:1], ACT.Exp).then_inc(eps_read, 1)
                    act.wait_ge(qbias_set, l)
                for n in range(len(UNITS[l])):
                    if l == 0 and n == 4:
                        act.wait_ge(v_zero, 1)
                    project_out(l, n)
                for s in range(STEPS):
                    probabilities(l, s)
                    if s % TILES == LAG - 1 and s > TILES:
                        pv_out(l, s // TILES - 1)
                pv_out(l, NH - 1)
                if l < 2:
                    if l == 0:
                        act.wait_ge(const_set, 7)
                    else:
                        act.wait_ge(eps_read, 2)
                    act.activation(spare[:, 0:1], eps[:, 0:1], ACT.Sqrt).then_inc(eps_read, 1)
            act.wait_ge(row_in, 16)
            for c in range(2):
                act.wait_ge(ke_done, c + 1)
                act.activation(Ke[:, HALF * c:HALF * (c + 1)], B[0:L3_DIM, 2 + c, :], ACT.Identity,
                               bias=col[0:L3_DIM, BE:BE + 1]).then_inc(ke_used, 1)
            act.wait_ge(gate_sums, TILES)
            act.activation(gate[:, 1, :], gate[:, 0, :], ACT.Exp, scale=-1.0 / 128).then_inc(sd_ready, 1)
            act.wait_ge(max_ready, 1)
            for c in range(KC):
                act.activation(energy[:, 0, c, :], M[:, L3_DIM * c:L3_DIM * (c + 1)], ACT.Exp,
                               bias=esum[:, 0, c:c + 1], accum_out=esum[:, 1, c:c + 1]).then_inc(sd_ready, 1)

        @block.vector
        def _(dve):
            chain = [0]

            def link(ins):
                chain[0] += 1
                ins.then_inc(dve_chain, 1)
                dve.wait_ge(dve_chain, chain[0])

            dve.wait_ge(pos_dma, 16)
            pv_rows = pos_v[:, :, :].rearrange("p (y two) x -> p y two x", two=2)
            tmp_rows = pos_t[:, :, :].rearrange("p (y two) x -> p y two x", two=2)
            link(dve.tensor_scalar(pos_t[:, 0:RES, :], pos_in[:, :, :], 0.25, None, ALU.mult))
            link(dve.tensor_scalar(pos_t[:, RES:2 * RES, :], pos_in[:, :, :], 0.75, None, ALU.mult))
            quarter, most = pos_t[:, 0:RES, :], pos_t[:, RES:2 * RES, :]
            link(dve.tensor_tensor(pv_rows[:, 1:RES, 0, :], most[:, 1:RES, :], quarter[:, 0:RES - 1, :], ALU.add))
            link(dve.tensor_tensor(pv_rows[:, 0:RES - 1, 1, :], most[:, 0:RES - 1, :], quarter[:, 1:RES, :], ALU.add))
            link(dve.tensor_copy(pv_rows[:, 0, 0, :], pos_in[:, 0, :]))
            link(dve.tensor_copy(pv_rows[:, RES - 1, 1, :], pos_in[:, RES - 1, :]))
            pos_x = pos.rearrange("p (y x two) -> p y x two", y=2 * RES, two=2)
            link(dve.tensor_scalar(pos_t[:, :, :], pos_v[:, :, :], 0.25, None, ALU.mult))
            link(dve.scalar_tensor_tensor(out=pos_x[:, :, 1:RES, 0], in0=pos_v[:, :, 1:RES], scalar=0.75,
                                          in1=pos_t[:, :, 0:RES - 1], op0=ALU.mult, op1=ALU.add))
            link(dve.scalar_tensor_tensor(out=pos_x[:, :, 0:RES - 1, 1], in0=pos_v[:, :, 0:RES - 1], scalar=0.75,
                                          in1=pos_t[:, :, 1:RES], op0=ALU.mult, op1=ALU.add))
            link(dve.tensor_copy(pos_x[:, :, 0, 0], pos_v[:, :, 0]))
            link(dve.tensor_copy(pos_x[:, :, RES - 1, 1], pos_v[:, :, RES - 1]))
            dve.tensor_copy(posH[:, :], pos).then_inc(pos_ready, 1)
            dve.wait_ge(pos_ready, 2)
            dve.tensor_tensor(posL[:, :], pos, posH[:, :].bitcast(F32), ALU.subtract).then_inc(pos_ready, 1)
            dve.wait_ge(cols_in, 16)

            def split(l, n):
                kind, c, half = UNITS[l][n]
                i = qk_index(l, n)
                cols_ = slice(HALF * half, HALF * (half + 1))
                dve.wait_ge(proj_used, UNIT0[l] + n + 1)
                dve.tensor_tensor((qL if kind == "q" else kL)[:, c, cols_], q_full[:, i % 4, :],
                                  (qH if kind == "q" else kH)[:, c, cols_].bitcast(F32),
                                  ALU.subtract).then_inc(split_ready, 1)

            def maxima(l, a):
                n = l * NH + a // TILES
                for half in range(2):
                    u = 2 * (l * STEPS + a) + half
                    dve.wait_ge(a_done, u + 1)
                    if a % TILES == 0 and half == 0 and n >= 2:
                        dve.wait_ge(negmax_ready, n - 1)
                    dve.tensor_reduce(max16[:, n % 2, half * TILES + a % TILES:half * TILES + a % TILES + 1],
                                      A[:, u % 2, :], AX.X, ALU.max, negate=True).then_inc(a_used, 1)
                if a % TILES == TILES - 1:
                    dve.wait_ge(a_used, 2 * (l * STEPS + a + 1))
                    if n >= 2:
                        dve.wait_ge(rows_done, n - 1)
                    dve.tensor_tensor(negmax[:, n % 2, :], max16[:, n % 2, 0:TILES],
                                      max16[:, n % 2, TILES:2 * TILES], ALU.min).then_inc(negmax_ready, 1)

            def max_rows(l, h):
                n = l * NH + h
                dve.wait_ge(rows_done, n + 1)
                if n >= 2:
                    dve.wait_ge(shift_dma[n % 2], 32 * (n // 2))
                dve.tensor_copy(mH[:, n % 2, :], M[0:TILES, 0:P]).then_inc(rows_used, 1)
                dve.wait_ge(rows_used, 2 * n + 1)
                dve.tensor_tensor(mL[:, n % 2, :], M[0:TILES, 0:P], mH[:, n % 2, :].bitcast(F32),
                                  ALU.subtract).then_inc(rows_used, 1)

            def reciprocals(l, pair, part):
                n = l * NH + 2 * pair
                if part == 0:
                    dve.wait_ge(pv_used, 2 * (n + 2))
                    dve.wait_ge(att_ready, 2 * n)
                    if l and pair == 0:
                        dve.wait_ge(att_tail, 2 * l)
                cs = slice(HALF // REC_PARTS * part, HALF // REC_PARTS * (part + 1))
                dve.reciprocal(rec_sb[:, cs], den_sb[:, pair % 2, cs]).then_inc(rec_ready, 1)

            def last_heads(l):
                n = l * NH + NH - 2
                dve.wait_ge(pv_used, 2 * (n + 1))
                dve.wait_ge(att_ready, 2 * (n - 1))
                dve.reciprocal(rec_sb[0:64, :], den_sb[0:64, 1, :]).then_inc(rec_ready, 1)
                dve.wait_ge(pv_used, 2 * (n + 2))
                dve.wait_ge(att_ready, 2 * n)
                for part in range(2):
                    cs = slice(QUARTER * part, QUARTER * (part + 1))
                    dve.reciprocal(rec_sb[64:128, cs], den_sb[64:128, 1, cs]).then_inc(rec_ready, 1)
                dve.wait_ge(rec_ready, REC_LAYER * (l + 1))
                for half in range(2):
                    src = slice(64 + DP * half, 64 + DP * half + DP)
                    dve.tensor_tensor(att[P - DP:P, KC - 1, HALF * half + QUARTER:HALF * (half + 1)],
                                      pv_sb[src, 1, QUARTER:HALF], rec_sb[src, QUARTER:HALF],
                                      ALU.mult).then_inc(att_tail, 1)

            def group_norm(l):
                g = gsmall
                dve.wait_ge(stats_in, 4 * l)
                for c in range(KC):
                    dve.bn_aggr(mv[:, c, :], stats[:, c, :, :].rearrange("p a b -> p (a b)")).then_inc(stat_ready, 1)
                dve.wait_ge(stat_ready, 3 * l - 1)
                dve.wait_ge(stat_done, 2 * l - 1)
                link(dve.tensor_tensor(g[:, 1, :], mv[:, :, 0], M[:, 2:4], ALU.subtract))
                link(dve.tensor_tensor(g[:, 2, :], g[:, 1, :], g[:, 1, :], ALU.mult))
                dve.tensor_tensor(g[:, 3, :], g[:, 2, :], mv[:, :, 1], ALU.add).then_inc(stat_ready, 1)
                dve.wait_ge(sd_ready, l + 1)
                link(dve.reciprocal(g[:, 5, :], g[:, 4, :]))
                link(dve.tensor_tensor(g[:, 5, :], g[:, 5, :], col[:, GAM[l][0]:GAM[l][1] + 1], ALU.mult))
                link(dve.tensor_tensor(g[:, 6, :], g[:, 5, :], M[:, 2:4], ALU.mult))
                link(dve.tensor_tensor(g[:, 6, :], col[:, BET[l][0]:BET[l][1] + 1], g[:, 6, :], ALU.subtract))
                for c in range(KC):
                    dve.tensor_scalar(XN[:, c, :], X[:, c, :], g[:, 5, c:c + 1], g[:, 6, c:c + 1],
                                      ALU.mult, ALU.add).then_inc(xn_ready, 1)
                dve.tensor_scalar(qbias[:, :], col[:, BQ[l][0]:BQ[l][1] + 1], float(HEAD_DIM[l]) ** -0.5, None,
                                  ALU.mult).then_inc(qbias_set, 1)

            def unit_stats(u):
                dve.bn_stats(stats[:, u // 2, u % 2, :],
                             X[:, u // 2, HALF * (u % 2):HALF * (u % 2 + 1)]).then_inc(stats_in, 1)

            for l in range(LAYERS):
                if l:
                    group_norm(l)
                n_units = len(UNITS[l])
                late = set(LATE[l].values())
                for n in range(n_units):
                    if UNITS[l][n][0] != "v" and n not in late:
                        split(l, n)
                for a in range(LEAD):
                    maxima(l, a)
                    if a in LATE[l]:
                        split(l, LATE[l][a])
                    if a == TILES - 1:
                        max_rows(l, 0)
                for s in range(STEPS):
                    a = s + LEAD
                    if s % TILES == TILES - 3 and s // TILES + 1 < NH:
                        max_rows(l, s // TILES + 1)
                    if a < STEPS:
                        maxima(l, a)
                    pair, part = (s - LAG - 1) // (2 * TILES) - 1, (s - LAG - 1) % (2 * TILES)
                    if 0 <= pair and part < REC_PARTS:
                        reciprocals(l, pair, part)
                last_heads(l)
                if l == 0:
                    link(dve.tensor_copy(obias[:, :], col[:, B_PROJ[0][0]:B_PROJ[0][1] + 1]))
                else:
                    dve.wait_ge(vb_done, l)
                    link(dve.tensor_tensor(obias[:, :], M[:, 0:2], col[:, B_PROJ[l][0]:B_PROJ[l][1] + 1], ALU.add))
                for i, u in enumerate(UNIT_ORDER):
                    c, half = u // 2, u % 2
                    cs = slice(HALF * half, HALF * (half + 1))
                    dve.wait_ge(out_done, 4 * l + i + 1)
                    dve.scalar_tensor_tensor(out=X[:, c, cs], in0=B[:, u, :], scalar=obias[:, c:c + 1],
                                             in1=X[:, c, cs], op0=ALU.add, op1=ALU.add).then_inc(x_ready, 1)
                    if l == 1 and i:
                        dve.wait_ge(x_ready, 4 * l + i)
                        unit_stats(UNIT_ORDER[i - 1])
                dve.wait_ge(x_ready, 4 * (l + 1))
                if l == 1:
                    unit_stats(UNIT_ORDER[3])
                if l == 0:
                    for i, u in enumerate(UNIT_ORDER):
                        c, half = u // 2, u % 2
                        cs = slice(HALF * half, HALF * (half + 1))
                        dve.wait_ge(ln_done, half + 1)
                        dve.tensor_tensor(att[:, c, cs], X[:, c, cs], A[:, half, :], ALU.subtract).then_inc(ln_in, 1)
                    dve.wait_ge(sd_ready, 1)
                    dve.reciprocal(rstd8[:, 1, :], rstd8[:, 0, :]).then_inc(rstd_ready, 1)
                    dve.wait_ge(ln_in, 4)
                    for i, u in enumerate(UNIT_ORDER):
                        c, half = u // 2, u % 2
                        cs = slice(HALF * half, HALF * (half + 1))
                        dve.wait_ge(ln_done, 4 + half)
                        dve.tensor_tensor(X[:, c, cs], att[:, c, cs], B[:, half, :], ALU.mult).then_inc(ln_scaled, 1)
                        if i >= 2:
                            dve.wait_ge(ln_out, i - 1)
                            unit_stats(UNIT_ORDER[i - 2])
                    for i in (2, 3):
                        dve.wait_ge(ln_out, i + 1)
                        unit_stats(UNIT_ORDER[i])
            dve.wait_ge(row_in, 16)
            for t in range(TILES):
                b = t % 2
                dve.wait_ge(t_done, t + 1)
                dve.tensor_tensor(QKV3[:, t, :], B[:, b, :], bias3[:, 0:HALF], ALU.add).then_inc(dve_chain, 1)
                chain[0] += 1
                dve.tensor_tensor(QS3[:, t, :], A[:, b, 0:L3_DIM], bias3[:, HALF:L3_COLS],
                                  ALU.add).then_inc(t_used, 1)
                dve.wait_ge(dve_chain, chain[0])
                link(dve.tensor_tensor(QK3[:, t, :], QKV3[:, t, 0:P], QKV3[:, t, P:2 * P], ALU.mult))
                dve.tensor_reduce(gate[:, 0, t:t + 1], QK3[:, t, :], AX.X, ALU.add).then_inc(gate_sums, 1)
            dve.wait_ge(sd_ready, 4)
            link(dve.tensor_scalar(gate[:, 2, :], gate[:, 1, :], 1.0, None, ALU.add))
            link(dve.reciprocal(gate[:, 3, :], gate[:, 2, :]))
            for t in range(TILES):
                dve.tensor_scalar(QS3[:, t, :], QS3[:, t, :], gate[:, 3, t:t + 1], None,
                                  ALU.mult).then_inc(qs_ready, 1)
            dve.wait_ge(en_done, 1)
            dve.tensor_reduce(esum[:, 0, :], M[:, 0:KC * L3_DIM].rearrange("p (c d) -> p c d", c=KC), AX.X, ALU.max,
                              negate=True).then_inc(max_ready, 1)
            dve.wait_ge(sd_ready, 6)
            link(dve.reciprocal(esum[:, 2, :], esum[:, 1, :]))
            for c in range(KC):
                dve.tensor_scalar(energy[:, 1, c, :], energy[:, 0, c, :], esum[:, 2, c:c + 1], None,
                                  ALU.mult).then_inc(attn3, 1)
            dve.wait_ge(at_done, 1)
            dve.tensor_copy(attT[:, :], M[0:L3_DIM, 0:C]).then_inc(at_used, 1)
            for u in range(4):
                c, half = u // 2, u % 2
                cs = slice(HALF * half, HALF * (half + 1))
                dve.wait_ge(vo_done, u + 1)
                dve.tensor_tensor(XN[:, c, cs], B[:, u, :], X[:, c, cs], ALU.add).then_inc(fin_ready, 1)

        @block.tensor
        def _(pe):
            def projection(l, n):
                kind, c, half = UNITS[l][n]
                u = UNIT0[l] + n
                src = X if l == 0 else XN
                if n >= 4:
                    pe.wait_ge(proj_used, u - 3)
                if kind == "v":
                    t, tiles = c, half
                    wide = HALF // tiles
                    for j in range(tiles):
                        for kc in range(KC):
                            mm = pe.matmul(B[:, u % 4, wide * j:wide * (j + 1)],
                                           src[:, kc, P * (t + j):P * (t + j + 1)],
                                           W[l][:, kc, 2 * wide:3 * wide], start=(kc == 0), stop=(kc == KC - 1))
                else:
                    wide = P if l == 0 else C
                    off = (0 if kind == "q" else wide) + P * c
                    for kc in range(KC):
                        mm = pe.matmul(B[:, u % 4, :], W[l][:, kc, off:off + P],
                                       src[:, kc, HALF * half:HALF * (half + 1)],
                                       start=(kc == 0), stop=(kc == KC - 1))
                mm.then_inc(proj_done, 1)

            def scores_for_max(l, a):
                h, t = a // TILES, a % TILES
                if t == 0:
                    pe.wait_ge(stack_dma[h], stack_count(l))
                for half in range(2):
                    u = 2 * (l * STEPS + a) + half
                    if u >= 2:
                        pe.wait_ge(a_used, u - 1)
                    pe.matmul(A[:, u % 2, :], q_stack[0:SPLIT_ROWS[l], h, P * t:P * (t + 1)],
                              k_stack[0:SPLIT_ROWS[l], h, HALF * half:HALF * (half + 1)],
                              start=True, stop=True).then_inc(a_done, 1)

            def transpose_max(l, h):
                n = l * NH + h
                pe.wait_ge(negmax_ready, n + 1)
                if n:
                    pe.wait_ge(rows_used, 2 * n)
                pe.transpose(M[0:TILES, 0:P], negmax[:, n % 2, :], ident[:, :]).then_inc(rows_done, 1)

            def scores(l, s):
                g = l * STEPS + s
                h, t = s // TILES, s % TILES
                if t == 0:
                    n = l * NH + h
                    pe.wait_ge(shift_dma[n % 2], 32 * (n // 2 + 1))
                if g >= 2:
                    pe.wait_ge(e_ready, g - 1)
                for half in range(2):
                    mm = pe.matmul(B[:, 2 * (g % 2) + half, :], k_stack[0:SHIFT_ROWS[l], h, P * t:P * (t + 1)],
                                   q_stack[0:SHIFT_ROWS[l], h, HALF * half:HALF * (half + 1)],
                                   start=True, stop=True)
                mm.then_inc(b_done, 1)

            def values(l, s):
                g = l * STEPS + s
                h, t = s // TILES, s % TILES
                n = l * NH + h
                pe.wait_ge(e_ready, g + 1)
                if t == 0 and n:
                    pe.wait_ge(pv_used, 2 * n)
                for part, lhs in enumerate((V[:, t, DP * h:DP * (h + 1)], ones[:, 0:DP])):
                    for half in range(2):
                        r = 64 * part + DP * half
                        mm = pe.matmul(PV[r:r + DP, :], lhs, E[:, g % E_BUFS, HALF * half:HALF * (half + 1)],
                                       start=(t == 0), stop=(t == TILES - 1))
                mm.then_inc(pv_done, 1)

            pe.wait_ge(const_set, 7)
            for l in range(LAYERS):
                pe.wait_ge(w_in[l], 16)
                if l == 0:
                    pe.wait_ge(x_in, 16 * KC)
                else:
                    pe.wait_ge(stat_ready, 3 * l - 1)
                    pe.matmul(M[:, 2:4], group_avg[:, :], mv[:, :, 0], start=True, stop=True).then_inc(stat_done, 1)
                    pe.wait_ge(stat_ready, 3 * l)
                    pe.matmul(M[:, 4:6], group_avg[:, :], gsmall[:, 3, :], start=True, stop=True).then_inc(stat_done, 1)
                    pe.wait_ge(xn_ready, 2 * l)
                late = set(LATE[l].values())
                for n in range(len(UNITS[l])):
                    if n not in late:
                        projection(l, n)
                if l == 0:
                    pe.wait_ge(pos_rows, 16 * 12)
                for a in range(LEAD):
                    scores_for_max(l, a)
                    if a in LATE[l]:
                        projection(l, LATE[l][a])
                    if a == TILES - 1:
                        transpose_max(l, 0)
                pe.wait_ge(proj_used, UNIT0[l] + len(UNITS[l]))
                for s in range(0, STEPS, 2):
                    scores(l, s)
                    scores(l, s + 1)
                    if s + LEAD < STEPS:
                        scores_for_max(l, s + LEAD)
                    if s >= LAG:
                        values(l, s - LAG)
                        values(l, s - LAG + 1)
                    if s % TILES == TILES - 4 and s // TILES + 1 < NH:
                        transpose_max(l, s // TILES + 1)
                    if s + LEAD < STEPS:
                        scores_for_max(l, s + LEAD + 1)
                for s in range(STEPS - LAG, STEPS):
                    values(l, s)
                wo = (W_COLS[l] - C)
                if l:
                    for c in range(KC):
                        for kc in range(KC):
                            mm = pe.matmul(M[:, c:c + 1], W[l][:, kc, wo + P * c:wo + P * (c + 1)],
                                           col[:, BV[l][kc]:BV[l][kc] + 1], start=(kc == 0), stop=(kc == KC - 1))
                    mm.then_inc(vb_done, 1)
                pe.wait_ge(e_ready, STEPS * (l + 1))
                for kc in range(KC):
                    pe.wait_ge(att_ready, 2 * (l * NH + 4 * (kc + 1)))
                    if kc == KC - 1:
                        pe.wait_ge(att_tail, 2 * (l + 1))
                    for u in UNIT_ORDER:
                        c, half = u // 2, u % 2
                        mm = pe.matmul(B[:, u, :], W[l][:, kc, wo + P * c:wo + P * (c + 1)],
                                       att[:, kc, HALF * half:HALF * (half + 1)], start=(kc == 0), stop=(kc == KC - 1))
                        if kc == KC - 1:
                            mm.then_inc(out_done, 1)
                if l == 0:
                    for half in range(2):
                        pe.wait_ge(x_ready, 2 * (half + 1))
                        for kc in range(KC):
                            mm = pe.matmul(A[:, half, :], chan_avg[:, :], X[:, kc, HALF * half:HALF * (half + 1)],
                                           start=(kc == 0), stop=(kc == KC - 1))
                        mm.then_inc(ln_done, 1)
                    for t in range(TILES):
                        if t % 4 == 0:
                            pe.wait_ge(sq_ready, 2 + 2 * (t // 4))
                        for kc in range(KC):
                            mm = pe.matmul(M[:, 8 + t:9 + t], XN[:, kc, P * t:P * (t + 1)], chan_avg[:, 0:1],
                                           start=(kc == 0), stop=(kc == KC - 1))
                    mm.then_inc(ln_done, 1)
                    pe.wait_ge(rstd_ready, 1)
                    for t in range(TILES):
                        mm = pe.matmul(B[:, t // 4, P * (t % 4):P * (t % 4 + 1)],
                                       rstd8[:, 1, t:t + 1].to_broadcast([P, P]), ident[:, :], start=True, stop=True)
                        if t % 4 == 3:
                            mm.then_inc(ln_done, 1)
            pe.wait_ge(w_in[3], 16)
            pe.wait_ge(x_ready, 4 * LAYERS)
            for c in range(2):
                for kc in range(KC):
                    mm = pe.matmul(B[0:L3_DIM, 2 + c, :], W3[:, kc, L3_COLS:L3_COLS + L3_DIM],
                                   X[:, kc, HALF * c:HALF * (c + 1)], start=(kc == 0), stop=(kc == KC - 1))
                mm.then_inc(ke_done, 1)
            for t in range(TILES):
                b = t % 2
                if t >= 2:
                    pe.wait_ge(t_used, t - 1)
                for kc in range(KC):
                    pe.matmul(B[:, b, :], X[:, kc, P * t:P * (t + 1)], W3[:, kc, 0:HALF],
                              start=(kc == 0), stop=(kc == KC - 1))
                for kc in range(KC):
                    mm = pe.matmul(A[:, b, 0:L3_DIM], X[:, kc, P * t:P * (t + 1)], W3[:, kc, HALF:L3_COLS],
                                   start=(kc == 0), stop=(kc == KC - 1))
                mm.then_inc(t_done, 1)
            for c in range(KC):
                for t in range(TILES):
                    if c == 0:
                        pe.wait_ge(qs_ready, t + 1)
                    mm = pe.matmul(M[:, L3_DIM * c:L3_DIM * (c + 1)], QKV3[:, t, 256 + P * c:256 + P * (c + 1)],
                                   QS3[:, t, :], start=(t == 0), stop=(t == TILES - 1))
            mm.then_inc(en_done, 1)
            for c in range(KC):
                pe.wait_ge(attn3, c + 1)
                mm = pe.transpose(M[0:L3_DIM, P * c:P * (c + 1)], energy[:, 1, c, :], ident[:, :])
            mm.then_inc(at_done, 1)
            pe.wait_ge(at_used, 1)
            pe.wait_ge(ke_used, 2)
            for u in range(4):
                c, half = u // 2, u % 2
                pe.matmul(B[:, u, :], attT[:, P * c:P * (c + 1)], Ke[:, HALF * half:HALF * (half + 1)],
                          start=True, stop=True).then_inc(vo_done, 1)


def kernel(**inputs):
    import numpy as np
    from concourse import bacc
    from concourse.bass_utils import run_bass_kernel_spmd

    g = {k: np.ascontiguousarray(v) for k, v in inputs.items()}

    def chunks(w):
        return np.ascontiguousarray(w.reshape(KC, P, -1).transpose(1, 0, 2))

    wp0 = np.zeros((NH, DP, C), np.float32)
    wp0[:, 0:16] = g["L0_conv_w_proj"].T.reshape(NH, 16, C)
    w0 = chunks(np.concatenate([g["L0_conv_w_qkv"].T, wp0.reshape(NH * DP, C)], 1))
    w1 = chunks(np.concatenate([g[f"L1_conv_w{n}"].T for n in "qkvo"], 1))
    w2 = chunks(np.concatenate([g["L2_conv_w_qkv"].T, g["L2_conv_w_proj"].T], 1))
    w3 = chunks(np.concatenate([g[f"L3_conv_W{n}"].T for n in "qkvse"], 1))
    vectors = [g["L0_conv_b_proj"], g["L0_conv_gamma"], g["L0_conv_beta"],
               g["L1_conv_bq"], g["L1_conv_bk"], g["L1_conv_bv"],
               g["L1_conv_bo"], g["L1_conv_gn_gamma"], g["L1_conv_gn_beta"],
               g["L2_conv_b_qkv"][0:C], g["L2_conv_b_qkv"][C:2 * C], g["L2_conv_b_qkv"][2 * C:],
               g["L2_conv_b_proj"], g["L2_conv_gamma"], g["L2_conv_beta"]]
    cols = np.zeros((P, 40), np.float32)
    for i, v in enumerate(vectors):
        cols[:, 2 * i:2 * i + 2] = v.reshape(KC, P).T
    cols[0:L3_DIM, 30] = g["L3_conv_be"]
    row3 = np.concatenate([g[f"L3_conv_b{n}"] for n in "qkvs"])[None, :]
    arrays = {"x_in_dram": g["x"].reshape(KC, P, N), "w0_dram": w0, "w1_dram": w1, "w2_dram": w2, "w3_dram": w3,
              "pos_dram": g["L0_conv_pos_bias"], "cols_dram": cols, "row3_dram": row3}
    nc = bacc.Bacc("TRN2", target_bir_lowering=False, num_devices=1)
    args = [nc.dram_tensor(n, a.shape, mybir.dt.from_np(a.dtype), kind="ExternalInput").ap() for n, a in arrays.items()]
    out = nc.dram_tensor("out_dram", (KC, P, N), F32, kind="ExternalOutput").ap()
    attention_chain(nc, *args, out)
    r = run_bass_kernel_spmd(nc, [arrays], core_ids=[0])
    return r.results[0]["out_dram"].reshape(1, C, 32, 32)
```

```python
from contextlib import ExitStack

import concourse.bass as bass
from concourse import mybir

F32 = mybir.dt.float32
F32R = mybir.dt.float32r
ALU = mybir.AluOpType
ACT = mybir.ActivationFunctionType
AX = mybir.AxisListType

P = 128
C = 256
KC = C // P
N = 1024
HALF = 512
NH = 8
TILES = N // P
DP = 32
LEAD = (14, 12, 12)
LAG = 2
STEPS = NH * TILES
E_BUFS = 4
LAYERS = 3
HEAD_DIM = (16, 32, 32)
POS_ROWS = 4
SPLIT_ROWS = tuple(3 * d + (POS_ROWS if d == 16 else 0) for d in HEAD_DIM)
SHIFT_ROW = P - 2
RING = 3
REC_PARTS = 8
NORM_GROUP = 8
EPS_LN = 1e-5
EPS_GN = (None, 1e5, 1e-5)
L3_DIM = 32
L3_QKS = 128 + 128 + L3_DIM
L3_COLS = L3_QKS + C
L3_STACK = 3 * L3_DIM
RES = 16
W_COLS = (3 * 128 + C, 4 * C, 4 * C)


def attention_chain(nc, x, w0, w1, w2, w3, pos_bias, cols, row3, out):
    ctx = ExitStack()
    with ctx:
        def sb(name, shape, dt=F32):
            return ctx.enter_context(nc.sbuf_tensor(name, shape, dt))

        def sem(name):
            return ctx.enter_context(nc.semaphore(name))

        X = sb("X", [P, KC, N])
        XN = sb("XN", [P, KC, N])
        q_full = sb("q_full", [P, 4, HALF])
        qH = sb("qH", [P, 2, N], F32R)
        qL = sb("qL", [P, 2, N], F32R)
        kH = sb("kH", [P, 2, N], F32R)
        kL = sb("kL", [P, 2, N], F32R)
        q_stack = sb("q_stack", [P, NH, N], F32R)
        k_stack = sb("k_stack", [P, NH, N], F32R)
        V = sb("V", [P, TILES, NH * DP])
        E = sb("E", [P, E_BUFS, N])
        ones = sb("ones", [P, P])
        att = sb("att", [P, KC, N])
        pv_sb = sb("pv_sb", [P, 2, HALF])
        den_sb = sb("den_sb", [P, 2, HALF])
        rec_sb = sb("rec_sb", [P, HALF])
        W = [sb(f"W{l}", [P, KC, W_COLS[l]]) for l in range(LAYERS)]
        W3 = sb("W3", [P, KC, L3_COLS + L3_STACK])
        col = sb("col", [P, 40])
        max16 = sb("max16", [P, 2, 2 * TILES])
        negmax = sb("negmax", [P, 2, TILES])
        mH = sb("mH", [TILES, 2, P], F32R)
        mL = sb("mL", [TILES, 2, P], F32R)
        ident = sb("ident", [P, P])
        group_avg = sb("group_avg", [P, P])
        chan_avg = sb("chan_avg", [P, P])
        gather = sb("gather", [P, P])
        sums_sb = sb("sums_sb", [P, HALF])
        stats = sb("stats", [P, KC, 2, 6])
        rstd8 = sb("rstd8", [P, 2, TILES])
        spare = sb("spare", [P, 2])
        mv = sb("mv", [P, KC, 2])
        gsmall = sb("gsmall", [P, 8, KC])
        qbias = sb("qbias", [P, 2])
        obias = sb("obias", [P, KC])
        eps = sb("eps", [P, 3])
        posH = sb("posH", [NH, N], F32R)
        posL = sb("posL", [NH, N], F32R)
        bias3 = sb("bias3", [P, L3_COLS])
        gate = sb("gate", [P, 4, TILES])
        energy = sb("energy", [P, KC, L3_DIM])
        fold = sb("fold", [P, L3_DIM])
        esum = sb("esum", [P, 3, KC])
        pos_v = E[0:NH, 1, 0:HALF].rearrange("p (y x) -> p y x", x=RES)
        pos_t = E[0:NH, 1, HALF:N].rearrange("p (y x) -> p y x", x=RES)
        pos_in = E[0:NH, 3, 0:RES * RES].rearrange("p (y x) -> p y x", x=RES)
        pos = att[0:NH, 0, :]
        odd_den = W[0][0:64, 0, 0:HALF]
        odd_num = sums_sb[0:64, :]
        E_sum = [XN[:, 0, :], XN[:, 1, :]] + [q_full[:, 2 * k:2 * k + 2, :].rearrange("p a n -> p (a n)") for k in range(2)]
        XT = E[:, :, :].rearrange("p a n -> p (a n)")[:, 0:TILES * (C + 1)].rearrange("p (t c) -> p t c", t=TILES)
        QK = V
        QK_prod = pv_sb[:, :, :].rearrange("p a (t d) -> p (a t) d", d=P)
        QS = att[:, 0, 0:TILES * L3_DIM].rearrange("p (t d) -> p t d", t=TILES)
        G_sb = att[:, 0, HALF:HALF + 3 * L3_DIM]
        Ke = att[L3_DIM:2 * L3_DIM, 1, :]
        G_parts = den_sb[:, 0, 0:C + 1]
        soft = rec_sb[:, 0:KC * L3_STACK].rearrange("p (c r d) -> p c r d", c=KC, r=3)
        ke_stack = q_stack[0:L3_STACK, 0, :]
        at_stack = q_stack[0:L3_STACK, 1, 0:C]

        S = ctx.enter_context(nc.psum_tensor("S", [P, 2 * RING, HALF], F32))
        B = S[:, 0:RING, :]
        A = S[:, RING:2 * RING, :]
        PV = ctx.enter_context(nc.psum_tensor("PV", [P, HALF], F32))
        M = ctx.enter_context(nc.psum_tensor("M", [P, HALF], F32))

        B_PROJ, GAM, BET = [(0, 1), (12, 13), (24, 25)], [(2, 3), (14, 15), (26, 27)], [(4, 5), (16, 17), (28, 29)]
        BQ, BK, BV = [None, (6, 7), (18, 19)], [None, (8, 9), (20, 21)], [None, (10, 11), (22, 23)]
        BE = 30

        x_in, cols_in, w_in, w_v, pos_dma, row_in, out_dma = ([sem(f"x_in{i}") for i in range(2)], sem("cols_in"),
                                                         [sem(f"w_in{l}") for l in range(4)], sem("w_v"),
                                                         sem("pos_dma"), sem("row_in"), sem("out_dma"))
        const_set, ones_set, v_ones = sem("const_set"), sem("ones_set"), sem("v_ones")
        pool_chain, dve_chain = sem("pool_chain"), sem("dve_chain")
        pos_ready, pos_rows, one_rows_in, stacks_clear = sem("pos_ready"), sem("pos_rows"), sem("one_rows_in"), sem("stacks_clear")
        xn_ready = sem("xn_ready")
        qbias_set = sem("qbias_set")
        proj_done, proj_used = sem("proj_done"), sem("proj_used")
        high_ready = sem("high_ready")
        split_ready = sem("split_ready")
        stack_dma = [sem(f"stack_dma{h}") for h in range(NH)]
        a_done, a_used = sem("a_done"), sem("a_used")
        negmax_ready, rows_done, rows_used = sem("negmax_ready"), sem("rows_done"), sem("rows_used")
        shift_dma = [sem(f"shift_dma{i}") for i in range(2)]
        b_done, e_ready, pv_done, pv_used = sem("b_done"), sem("e_ready"), sem("pv_done"), sem("pv_used")
        sums_ready, gathered = sem("sums_ready"), sem("gathered")
        sum_ready, den_done, odd_ready = sem("sum_ready"), sem("den_done"), sem("odd_ready")
        rec_ready, att_ready, att_tail = sem("rec_ready"), sem("att_ready"), sem("att_tail")
        out_done, x_ready = sem("out_done"), sem("x_ready")
        stats_in, stat_ready, stat_done = sem("stats_in"), sem("stat_ready"), sem("stat_done")
        sd_ready = sem("sd_ready")
        vb_done = sem("vb_done")
        ln_in, ln_done, sq_ready = sem("ln_in"), sem("ln_done"), sem("sq_ready")
        rstd_ready, ln_scaled, ln_out, eps_read = sem("rstd_ready"), sem("ln_scaled"), sem("ln_out"), sem("eps_read")
        t_done, t_used, xt_done, xt_used = sem("t_done"), sem("t_used"), sem("xt_done"), sem("xt_used")
        gate_sums, gate_exp, qs_ready, fold_set = sem("gate_sums"), sem("gate_exp"), sem("qs_ready"), sem("fold_set")
        parts_done, parts_used, G_done, G_used = sem("parts_done"), sem("parts_used"), sem("G_done"), sem("G_used")
        en_done, max_ready, en_exp, soft_ready = sem("en_done"), sem("max_ready"), sem("en_exp"), sem("soft_ready")
        at_done, at_ready, ke_done, ke_used, ke_ready = (sem("at_done"), sem("at_ready"), sem("ke_done"), sem("ke_used"),
                                                         sem("ke_ready"))
        vo_done, fin_dve, fin_act = sem("vo_done"), sem("fin_dve"), sem("fin_act")

        UNITS = [[("q", 0, 0), ("q", 0, 1), ("k", 0, 0), ("k", 0, 1), ("v", 0, 4), ("v", 4, 4)]]
        for _ in range(2):
            UNITS.append([("q", 0, 0), ("q", 0, 1), ("k", 0, 0), ("k", 0, 1)] + [("v", t, 2) for t in (0, 2, 4, 6)]
                         + [("q", 1, 0), ("q", 1, 1), ("k", 1, 0), ("k", 1, 1)])
        UNIT0 = [sum(len(u) for u in UNITS[:l]) for l in range(LAYERS)]
        QK0 = [sum(sum(x[0] != "v" for x in u) for u in UNITS[:l]) for l in range(LAYERS)]

        def qk_index(l, n):
            return QK0[l] + sum(x[0] != "v" for x in UNITS[l][:n])

        LATE = [{}] + 2 * [{1: 7, 3: 8, 5: 9, 7: 10, 9: 11}]
        STACK_DMAS = 6

        def stack_count(l):
            return 16 * STACK_DMAS * (l + 1)

        REC_LAYER = 3 * REC_PARTS + 3

        def rec_count(l, h):
            return l * REC_LAYER + (REC_PARTS * (h // 2 + 1) if h < 6 else 3 * REC_PARTS + (1 if h == 6 else 3))

        def score_unit(i):
            return i // (2 * TILES), i // 2 % TILES, i % 2

        PAIRS = STEPS // 2
        SUMS = PAIRS - 1

        def sum_count(l, j):
            return (l - 1) * SUMS + j + 1

        def den_count(l, h, part):
            return 2 * ((l - 1) * NH + h) + part + 1

        def reciprocals_of(l, h):
            return W[0][:, 1, 0:HALF] if l and h >= NH - 2 else rec_sb

        ROWS_STEP = (2, 4, 4)

        p0 = SPLIT_ROWS[0] - POS_ROWS

        QKS_BANK, XT_BANK = (0, 2), (4, 5)
        KE_BANK = (1, 3)
        FINAL = (0, 2, 4, 5)

        UNIT_ORDER = (0, 2, 1, 3)
        QUARTER = HALF // 2

        block = ctx.enter_context(nc.Block())

        def head_source(l, h):
            return (0, 16 * h) if l == 0 else (h // 4, DP * (h % 4))

        def load_stack(eng, l, h, operands="qk", parts="HL"):
            c, p = head_source(l, h)
            rows = HEAD_DIM[l]
            blocks = {("q", "H"): (q_stack, qH, (0, 1)), ("q", "L"): (q_stack, qL, (2,)),
                      ("k", "H"): (k_stack, kH, (0, 2)), ("k", "L"): (k_stack, kL, (1,))}
            for name in operands:
                for part in parts:
                    stack, src, places = blocks[name, part]
                    for blk in places:
                        eng.dma_start(stack[rows * blk:rows * (blk + 1), h, :].bitcast(F32),
                                      src[p:p + rows, c, :].bitcast(F32)).then_inc(stack_dma[h], 16)

        @block.sync
        def _(sp):
            sp.dma_start(W[0][:, :, 0:2 * P], w0[:, :, 0:2 * P]).then_inc(w_in[0], 16)
            for half in range(2):
                sp.dma_start(X[:, :, HALF * half:HALF * (half + 1)],
                             x[:, :, HALF * half:HALF * (half + 1)].rearrange("c p n -> p c n")).then_inc(x_in[half], 16)
            sp.dma_start(W[0][:, :, 2 * P:], w0[:, :, 2 * P:]).then_inc(w_v, 16)
            sp.dma_start(W[1][:, :, :], w1).then_inc(w_in[1], 16)
            sp.dma_start(W[2][:, :, :], w2).then_inc(w_in[2], 16)
            sp.dma_start(W3[:, :, :], w3).then_inc(w_in[3], 16)
            sp.dma_start(bias3[:, :], row3.to_broadcast([P, L3_COLS])).then_inc(row_in, 16)
            for part, src in enumerate((posH, posL)):
                sp.wait_ge(pos_ready, part + 1)
                if part == 0:
                    sp.wait_ge(stacks_clear, 3)
                for dst, r in ((q_stack, p0 + 2 + part), (k_stack, p0 + part)):
                    sp.dma_start(dst[r:r + 1, :, :].bitcast(F32), src[:, :].bitcast(F32)).then_inc(pos_rows, 16)

            def shift_rows(l, h):
                n = l * NH + h
                for r, src in ((0, mH), (1, mL)):
                    sp.wait_ge(rows_used, 2 * n + r + 1)
                    row = SHIFT_ROW + r
                    sp.dma_start(q_stack[row:row + 1, h, :].bitcast(F32)
                                 .rearrange("o (t c) -> o t c", t=TILES),
                                 src[:, n % 2, :].bitcast(F32)).then_inc(shift_dma[n % 2], 16)

            for l in range(LAYERS):
                if l:
                    sp.wait_ge(b_done, 2 * STEPS * l)
                for part, name in enumerate("qk"):
                    sp.wait_ge(high_ready, 4 * l + 2 * (part + 1))
                    load_stack(sp, l, 0, name, "H")
                    sp.wait_ge(split_ready, QK0[l] + 2 * (part + 1))
                    load_stack(sp, l, 0, name, "L")
                load_stack(sp, l, 1)
                for h in range(NH):
                    if h + 2 == 4 and l:
                        sp.wait_ge(split_ready, QK0[l] + 8)
                    if h + 2 < NH:
                        load_stack(sp, l, h + 2)
                    shift_rows(l, h)
            for n in range(4):
                sp.wait_ge(fin_act if n % 2 else fin_dve, n // 2 + 1)
                sp.dma_start(out[n // 2, :, HALF * (n % 2):HALF * (n % 2 + 1)],
                             XN[:, n // 2, HALF * (n % 2):HALF * (n % 2 + 1)]).then_inc(out_dma, 16)
            sp.wait_ge(out_dma, 64)

        @block.gpsimd
        def _(pool):
            pool.dma_start(pos_in[:, :, :], pos_bias[0]).then_inc(pos_dma, 16)
            pool.memset(ones[:, :], 1.0).then_inc(ones_set, 1)
            pool.memset(k_stack[:, :, :].bitcast(F32), 0.0).then_inc(stacks_clear, 1)
            pool.memset(ident[:, :], 0.0).then_inc(pool_chain, 1)
            pool.memset(group_avg[:, :], 1.0 / NORM_GROUP).then_inc(pool_chain, 1)
            pool.memset(chan_avg[:, :], 1.0 / C).then_inc(const_set, 1)
            pool.memset(gather[:, :], 0.0).then_inc(pool_chain, 1)
            pool.memset(eps[:, 0:1], EPS_LN).then_inc(const_set, 1)
            pool.memset(eps[:, 1:2], EPS_GN[1]).then_inc(const_set, 1)
            pool.memset(eps[:, 2:3], EPS_GN[2]).then_inc(const_set, 1)
            pool.wait_ge(pool_chain, 3)
            pool.affine_select(out=ident[:, :], in_=ident[:, :], compare_op=ALU.not_equal, fill=1.0, base=0,
                               pattern=[[-1, P]], channel_multiplier=1).then_inc(const_set, 1)
            for par in range(2):
                for part in range(2):
                    out_cols = gather[:, 64 * part:64 * (part + 1)].rearrange("p (g j) -> p g j", j=DP)
                    pool.affine_select(out=out_cols, in_=out_cols, compare_op=ALU.not_equal, fill=1.0,
                                       base=-64 * par - DP // 2 * part, pattern=[[-DP, 2], [part - 1, DP]],
                                       channel_multiplier=1).then_inc(pool_chain, 1)
                if par == 0:
                    pool.wait_ge(pool_chain, 5)
            ga = group_avg[:, :].rearrange("p (g j) -> p g j", j=NORM_GROUP)
            pool.affine_select(out=ga, in_=ga, compare_op=ALU.is_ge, fill=0.0, base=0,
                               pattern=[[-NORM_GROUP, P // NORM_GROUP], [0, NORM_GROUP]],
                               channel_multiplier=1).then_inc(pool_chain, 1)
            pool.wait_ge(pool_chain, 8)
            pool.affine_select(out=ga, in_=ga, compare_op=ALU.is_ge, fill=0.0, base=NORM_GROUP - 1,
                               pattern=[[NORM_GROUP, P // NORM_GROUP], [0, NORM_GROUP]],
                               channel_multiplier=-1).then_inc(const_set, 1)
            pool.memset(V[:, :, :], 1.0).then_inc(v_ones, 1)
            pool.wait_ge(stacks_clear, 3)
            for dst, r in ((q_stack, p0), (k_stack, p0 + 2), (k_stack, SHIFT_ROW)):
                pool.dma_start(dst[r:r + 2, :, :].bitcast(F32), ones[:, :]).then_inc(one_rows_in, 16)

            def normalise(l, h):
                n = l * NH + h
                r = 64 * (h % 2)
                last = h == NH - 1
                if last:
                    pool.wait_ge(pv_used, 2 * (n + 1))
                    pool.wait_ge(rec_ready, rec_count(l, h) - 1)
                else:
                    pool.wait_ge(rec_ready, rec_count(l, h))
                if h == 0 and l:
                    pool.wait_ge(out_done, 4 * l)
                wide = QUARTER if last else HALF
                for half in range(2):
                    src = slice(r + DP * half, r + DP * half + DP)
                    pool.tensor_tensor(att[DP * (h % 4):DP * (h % 4) + DP, h // 4, HALF * half:HALF * half + wide],
                                       pv_sb[src, h // 2 % 2, 0:wide], reciprocals_of(l, h)[src, 0:wide],
                                       ALU.mult).then_inc(att_ready, 1)

            for l in range(LAYERS):
                for unit in LATE[l].values():
                    kind, c, half = UNITS[l][unit]
                    if kind == "v":
                        continue
                    i, cols_ = qk_index(l, unit), slice(HALF * half, HALF * (half + 1))
                    pool.wait_ge(proj_used, UNIT0[l] + unit + 1)
                    pool.wait_ge(split_ready, i)
                    pool.tensor_tensor((qL if kind == "q" else kL)[:, c, cols_], q_full[:, i % 4, :],
                                       (qH if kind == "q" else kH)[:, c, cols_].bitcast(F32),
                                       ALU.subtract).then_inc(split_ready, 1)
                if l == 0:
                    for h in range(NH):
                        normalise(l, h)
                    continue
                pool.wait_ge(split_ready, QK0[l] + 8)
                done = l * NH
                for j in range(PAIRS):
                    if j < SUMS:
                        g, h, q = l * STEPS + 2 * j, j // 4, j % 4
                        pool.wait_ge(e_ready, 2 * (g + 2))
                        if done:
                            pool.wait_ge(att_ready, 2 * done)
                        if j >= 4:
                            pool.wait_ge(den_done, den_count(l, h - 1, q // 2))
                        pool.tensor_tensor(E_sum[q], E[:, g % E_BUFS, :], E[:, g % E_BUFS + 1, :], ALU.add).then_inc(sum_ready, 1)
                    if j >= 15 and j % 8 in (7, 0):
                        pool.wait_ge(sum_ready, sum_count(l, min(j, SUMS - 1)))
                        normalise(l, j // 4 - 3)
                        done += 1
                for h in (5, 6, 7):
                    normalise(l, h)

        @block.scalar
        def _(act):
            act.dma_start(col[:, :], cols).then_inc(cols_in, 16)
            act.wait_ge(ones_set, 1)
            act.activation(q_stack[:, NH // 2:NH, :],
                           ones[:, 0:1].to_broadcast([P, NH // 2 * N]).rearrange("p (h n) -> p h n", n=N),
                           ACT.Copy, scale=0.0).then_inc(stacks_clear, 1)

            def project_out(l, n):
                kind, c, half = UNITS[l][n]
                u = UNIT0[l] + n
                act.wait_ge(proj_done, u + 1)
                if kind == "v":
                    t, tiles = c, half
                    if l == 0:
                        act.activation(V[:, t:t + tiles, :].rearrange("p t (h d) -> p t h d", d=DP)[:, :, :, 0:16],
                                       B[:, u % RING, :].rearrange("p (t h d) -> p t h d", t=tiles, d=16),
                                       ACT.Copy).then_inc(proj_used, 1)
                    else:
                        act.activation(V[:, t:t + tiles, :], B[:, u % RING, :].rearrange("p (t d) -> p t d", t=tiles),
                                       ACT.Copy).then_inc(proj_used, 1)
                    return
                i = qk_index(l, n)
                high = (qH if kind == "q" else kH)[:, c, HALF * half:HALF * (half + 1)]
                scale = float(HEAD_DIM[l]) ** -0.5 if kind == "q" else 1.0
                bias = 0.0
                if l:
                    bias = qbias[:, c:c + 1] if kind == "q" else col[:, BK[l][c]:BK[l][c] + 1]
                if i >= 4:
                    act.wait_ge(split_ready, i - 3)
                late = n in LATE[l].values()
                first = act.activation(q_full[:, i % 4, :], B[:, u % RING, :], ACT.Identity, bias=bias, scale=scale)
                if late:
                    act.activation(high, B[:, u % RING, :], ACT.Identity, bias=bias, scale=scale).then_inc(proj_used, 1)
                else:
                    first.then_inc(proj_used, 1)

            def probabilities(l, i):
                h, t, half = score_unit(i)
                g, v = l * STEPS + i // 2, 2 * l * STEPS + i
                if g >= E_BUFS and half == 0:
                    act.wait_ge(pv_done, g + 1 - E_BUFS)
                    if l:
                        act.wait_ge(sum_ready, sum_count(l, i // 4 - 2) if i >= 8 else (l - 1) * SUMS)
                act.wait_ge(b_done, v + 1)
                act.activation(E[:, g % E_BUFS, HALF * half:HALF * (half + 1)], B[:, v % RING, :],
                               ACT.Exp).then_inc(e_ready, 1)

            def sums_out(h):
                act.wait_ge(pv_done, TILES * (h + 1))
                if h:
                    act.wait_ge(gathered, h)
                act.activation(sums_sb[:, :], PV[:, :], ACT.Copy).then_inc(sums_ready, 1)

            def pv_out(h):
                r, slot = 64 * (h % 2), h // 2 % 2
                act.wait_ge(gathered, h + 1)
                if h >= 4:
                    act.wait_ge(rec_ready, rec_count(0, h - 4))
                    act.wait_ge(att_ready, 2 * (h - 3))
                if h < NH - 1:
                    act.activation(den_sb[r:r + 64, slot, :], M[64:128, :], ACT.Copy).then_inc(pv_used, 1)
                act.activation(pv_sb[r:r + 64, slot, :], M[0:64, :], ACT.Copy).then_inc(pv_used, 1 if h < NH - 1 else 2)

            def odd_numerators(l, h):
                n = l * NH + h
                act.wait_ge(pv_done, TILES * (n + 1))
                act.wait_ge(pv_used, 2 * n)
                act.activation(odd_num, PV[64:128, :], ACT.Copy).then_inc(odd_ready, 1)

            def odd_denominators(l, h):
                act.wait_ge(den_done, den_count(l, h, 1))
                act.activation(odd_den[:, :], M[64:128, :], ACT.Copy).then_inc(odd_ready, 1)

            for l in range(LAYERS):
                if l == 1:
                    for i, u in enumerate(UNIT_ORDER):
                        cs = slice(HALF * (u % 2), HALF * (u % 2 + 1))
                        act.wait_ge(ln_in, i + 1)
                        act.activation(XN[:, u // 2, cs], att[:, u // 2, cs], ACT.Square).then_inc(sq_ready, 1)
                    act.wait_ge(ln_done, 3)
                    act.activation(rstd8[:, 0, :], M[:, 8:8 + TILES], ACT.Sqrt, bias=eps[:, 0:1]).then_inc(sd_ready, 1)
                    for i, u in enumerate(UNIT_ORDER):
                        c, cs = u // 2, slice(HALF * (u % 2), HALF * (u % 2 + 1))
                        act.wait_ge(ln_scaled, i + 1)
                        act.activation(X[:, c, cs], X[:, c, cs], ACT.Identity, scale=col[:, GAM[0][c]:GAM[0][c] + 1],
                                       bias=col[:, BET[0][c]:BET[0][c] + 1]).then_inc(ln_out, 1)
                if l:
                    act.wait_ge(stat_done, 2 * l)
                    act.activation(gsmall[:, 4, :], M[:, 4:6], ACT.Sqrt,
                                   bias=eps[:, l:l + 1]).then_inc(sd_ready, 1)
                    act.activation(spare[:, 1:2], eps[:, 0:1], ACT.Exp).then_inc(eps_read, 1)
                    act.wait_ge(qbias_set, l)
                for n in range(len(UNITS[l])):
                    if l == 0 and n == 4:
                        act.wait_ge(v_ones, 1)
                    project_out(l, n)
                for s in range(0, STEPS, 2):
                    h = s // TILES - 1
                    if s % TILES == 0 and s and l == 0:
                        sums_out(h)
                    for i in range(2 * s, 2 * s + 4):
                        probabilities(l, i)
                        if l and s and s % TILES == 0 and i % 4 == 1:
                            odd_numerators(l, h)
                    if l and s > TILES and s % TILES == 2:
                        odd_denominators(l, h)
                    if l == 0 and s % TILES == 4 and s > TILES:
                        pv_out(h)
                if l == 0:
                    sums_out(NH - 1)
                    pv_out(NH - 1)
                else:
                    odd_numerators(l, NH - 1)
                    odd_denominators(l, NH - 1)
                if l < 2:
                    if l == 0:
                        act.wait_ge(const_set, 6)
                    else:
                        act.wait_ge(eps_read, 2)
                    act.activation(spare[:, 0:1], eps[:, 0:1], ACT.Sqrt).then_inc(eps_read, 1)
            act.activation(XT[:, :, C:C + 1], ones[:, 0:TILES].rearrange("p (t o) -> p t o", o=1), ACT.Copy).then_inc(xt_used, 1)
            for t in range(TILES):
                act.wait_ge(xt_done, t + 1)
                act.activation(XT[:, t, 0:C], S[:, XT_BANK[t % 2], 0:C], ACT.Copy).then_inc(xt_used, 1)
            act.wait_ge(gate_sums, TILES)
            act.activation(gate[:, 1, :], gate[:, 0, :], ACT.Exp, scale=-1.0 / 128).then_inc(gate_exp, 1)

            def key_out(half):
                cs = slice(HALF * half, HALF * (half + 1))
                act.wait_ge(ke_done, half + 1)
                act.activation(Ke[:, cs], S[L3_DIM:2 * L3_DIM, KE_BANK[half], :], ACT.Identity,
                               bias=col[L3_DIM:2 * L3_DIM, BE:BE + 1]).then_inc(ke_used, 1)
                act.activation(ke_stack[:, cs], S[0:L3_STACK, KE_BANK[half], :], ACT.Identity,
                               bias=col[0:L3_STACK, BE:BE + 1]).then_inc(ke_used, 1)

            key_out(0)
            key_out(1)
            act.wait_ge(max_ready, 1)
            for c in range(KC):
                act.activation(energy[:, c, :], M[:, P + L3_DIM * c:P + L3_DIM * (c + 1)], ACT.Exp,
                               bias=esum[:, 0, c:c + 1], accum_out=esum[:, 1, c:c + 1]).then_inc(en_exp, 1)
            for u in (1, 3):
                act.wait_ge(vo_done, u + 1)
                act.activation(XN[:, u // 2, HALF:N], S[:, FINAL[u], :], ACT.Copy).then_inc(fin_act, 1)

        @block.vector
        def _(dve):
            chain = [0]

            def link(ins):
                chain[0] += 1
                ins.then_inc(dve_chain, 1)
                dve.wait_ge(dve_chain, chain[0])

            dve.memset(q_stack[:, 0:NH // 2, :].bitcast(F32), 0.0).then_inc(stacks_clear, 1)
            dve.wait_ge(pos_dma, 16)
            pv_rows = pos_v[:, :, :].rearrange("p (y two) x -> p y two x", two=2)
            tmp_rows = pos_t[:, :, :].rearrange("p (y two) x -> p y two x", two=2)
            link(dve.tensor_scalar(pos_t[:, 0:RES, :], pos_in[:, :, :], 0.25, None, ALU.mult))
            link(dve.tensor_scalar(pos_t[:, RES:2 * RES, :], pos_in[:, :, :], 0.75, None, ALU.mult))
            quarter, most = pos_t[:, 0:RES, :], pos_t[:, RES:2 * RES, :]
            link(dve.tensor_tensor(pv_rows[:, 1:RES, 0, :], most[:, 1:RES, :], quarter[:, 0:RES - 1, :], ALU.add))
            link(dve.tensor_tensor(pv_rows[:, 0:RES - 1, 1, :], most[:, 0:RES - 1, :], quarter[:, 1:RES, :], ALU.add))
            link(dve.tensor_copy(pv_rows[:, 0, 0, :], pos_in[:, 0, :]))
            link(dve.tensor_copy(pv_rows[:, RES - 1, 1, :], pos_in[:, RES - 1, :]))
            pos_x = pos.rearrange("p (y x two) -> p y x two", y=2 * RES, two=2)
            link(dve.tensor_scalar(pos_t[:, :, :], pos_v[:, :, :], 0.25, None, ALU.mult))
            link(dve.scalar_tensor_tensor(out=pos_x[:, :, 1:RES, 0], in0=pos_v[:, :, 1:RES], scalar=0.75,
                                          in1=pos_t[:, :, 0:RES - 1], op0=ALU.mult, op1=ALU.add))
            link(dve.scalar_tensor_tensor(out=pos_x[:, :, 0:RES - 1, 1], in0=pos_v[:, :, 0:RES - 1], scalar=0.75,
                                          in1=pos_t[:, :, 1:RES], op0=ALU.mult, op1=ALU.add))
            link(dve.tensor_copy(pos_x[:, :, 0, 0], pos_v[:, :, 0]))
            link(dve.tensor_copy(pos_x[:, :, RES - 1, 1], pos_v[:, :, RES - 1]))
            dve.tensor_copy(posH[:, :], pos).then_inc(pos_ready, 1)
            dve.wait_ge(pos_ready, 1)
            dve.tensor_tensor(posL[:, :], pos, posH[:, :].bitcast(F32), ALU.subtract).then_inc(pos_ready, 1)
            dve.wait_ge(cols_in, 16)

            def split(l, n):
                kind, c, half = UNITS[l][n]
                i = qk_index(l, n)
                cols_ = slice(HALF * half, HALF * (half + 1))
                dve.wait_ge(proj_used, UNIT0[l] + n + 1)
                if n not in LATE[l].values():
                    dve.tensor_copy((qH if kind == "q" else kH)[:, c, cols_], q_full[:, i % 4, :]).then_inc(high_ready, 1)
                    dve.wait_ge(high_ready, 4 * l + n + 1)
                dve.tensor_tensor((qL if kind == "q" else kL)[:, c, cols_], q_full[:, i % 4, :],
                                  (qH if kind == "q" else kH)[:, c, cols_].bitcast(F32),
                                  ALU.subtract).then_inc(split_ready, 1)

            def maxima(l, i):
                h, t, half = score_unit(i)
                n, u = l * NH + h, 2 * l * STEPS + i
                dve.wait_ge(a_done, u + 1)
                if t == 0 and half == 0 and n >= 2:
                    dve.wait_ge(negmax_ready, n - 1)
                dve.tensor_reduce(max16[:, n % 2, half * TILES + t:half * TILES + t + 1],
                                  A[:, u % RING, :], AX.X, ALU.max, negate=True).then_inc(a_used, 1)
                if t == TILES - 1 and half == 1:
                    dve.wait_ge(a_used, u + 1)
                    if n >= 2:
                        dve.wait_ge(rows_done, n - 1)
                    dve.tensor_tensor(negmax[:, n % 2, :], max16[:, n % 2, 0:TILES],
                                      max16[:, n % 2, TILES:2 * TILES], ALU.min).then_inc(negmax_ready, 1)

            def max_rows(l, h):
                n = l * NH + h
                dve.wait_ge(rows_done, n + 1)
                if n >= 2:
                    dve.wait_ge(shift_dma[n % 2], 32 * (n // 2))
                dve.tensor_copy(mH[:, n % 2, :], M[0:TILES, 0:P]).then_inc(rows_used, 1)
                dve.wait_ge(rows_used, 2 * n + 1)
                dve.tensor_tensor(mL[:, n % 2, :], M[0:TILES, 0:P], mH[:, n % 2, :].bitcast(F32),
                                  ALU.subtract).then_inc(rows_used, 1)

            def even_numerators(l, h):
                n, r, slot = l * NH + h, 64 * (h % 2), h // 2 % 2
                dve.wait_ge(odd_ready, den_count(l, h, 0))
                dve.wait_ge(att_ready, 2 * (n - 3))
                if h == 3:
                    dve.wait_ge(att_tail, 2 * l)
                dve.tensor_tensor(pv_sb[r:r + 64, slot, :], PV[0:64, :], odd_num, ALU.add).then_inc(pv_used, 1)

            def even_denominators(l, h):
                n, r, slot = l * NH + h, 64 * (h % 2), h // 2 % 2
                dve.wait_ge(odd_ready, den_count(l, h, 1))
                dve.wait_ge(rec_ready, rec_count(l, h - 4) if h >= 4 else rec_count(l - 1, h + NH - 4))
                dve.tensor_tensor(den_sb[r:r + 64, slot, :], M[0:64, :], odd_den[:, :], ALU.add).then_inc(pv_used, 1)

            def reciprocals(l, pair, part):
                n = l * NH + 2 * pair
                if part == 0:
                    dve.wait_ge(pv_used, 2 * (n + 2))
                    dve.wait_ge(att_ready, 2 * n)
                    if l and pair == 0:
                        dve.wait_ge(att_tail, 2 * l)
                cs = slice(HALF // REC_PARTS * part, HALF // REC_PARTS * (part + 1))
                dve.reciprocal(rec_sb[:, cs], den_sb[:, pair % 2, cs]).then_inc(rec_ready, 1)

            def last_heads(l):
                n = l * NH + NH - 2
                rec = reciprocals_of(l, NH - 1)
                if l:
                    dve.wait_ge(att_ready, 2 * NH * l)
                    dve.wait_ge(att_tail, 2 * l)
                else:
                    dve.wait_ge(att_ready, 2 * (n - 1))
                dve.wait_ge(pv_used, 2 * (n + 1))
                dve.reciprocal(rec[0:64, :], den_sb[0:64, 1, :]).then_inc(rec_ready, 1)
                if l:
                    even_numerators(l, NH - 1)
                    even_denominators(l, NH - 1)
                    dve.wait_ge(pv_used, 2 * (n + 2))
                else:
                    dve.wait_ge(gathered, NH)
                    dve.wait_ge(att_ready, 2 * n)
                for part in range(2):
                    cs = slice(QUARTER * part, QUARTER * (part + 1))
                    dve.reciprocal(rec[64:128, cs], den_sb[64:128, 1, cs] if l else M[64:128, cs]).then_inc(rec_ready, 1)
                dve.wait_ge(pv_used, 2 * (n + 2))
                dve.wait_ge(rec_ready, REC_LAYER * (l + 1))
                for half in range(2):
                    src = slice(64 + DP * half, 64 + DP * half + DP)
                    dve.tensor_tensor(att[P - DP:P, KC - 1, HALF * half + QUARTER:HALF * (half + 1)],
                                      pv_sb[src, 1, QUARTER:HALF], rec[src, QUARTER:HALF],
                                      ALU.mult).then_inc(att_tail, 1)

            def group_norm(l):
                g = gsmall
                dve.tensor_scalar(qbias[:, :], col[:, BQ[l][0]:BQ[l][1] + 1], float(HEAD_DIM[l]) ** -0.5, None,
                                  ALU.mult).then_inc(qbias_set, 1)
                dve.wait_ge(qbias_set, l)
                dve.wait_ge(stats_in, 4 * l)
                for c in range(KC):
                    dve.bn_aggr(mv[:, c, :], stats[:, c, :, :].rearrange("p a b -> p (a b)")).then_inc(stat_ready, 1)
                dve.wait_ge(stat_ready, 3 * l - 1)
                dve.wait_ge(stat_done, 2 * l - 1)
                link(dve.tensor_tensor(g[:, 1, :], mv[:, :, 0], M[:, 2:4], ALU.subtract))
                link(dve.tensor_tensor(g[:, 2, :], g[:, 1, :], g[:, 1, :], ALU.mult))
                dve.tensor_tensor(g[:, 3, :], g[:, 2, :], mv[:, :, 1], ALU.add).then_inc(stat_ready, 1)
                dve.wait_ge(sd_ready, l + 1)
                link(dve.reciprocal(g[:, 5, :], g[:, 4, :]))
                link(dve.tensor_tensor(g[:, 5, :], g[:, 5, :], col[:, GAM[l][0]:GAM[l][1] + 1], ALU.mult))
                link(dve.tensor_tensor(g[:, 6, :], g[:, 5, :], M[:, 2:4], ALU.mult))
                link(dve.tensor_tensor(g[:, 6, :], col[:, BET[l][0]:BET[l][1] + 1], g[:, 6, :], ALU.subtract))
                for u in UNIT_ORDER:
                    c, cs = u // 2, slice(HALF * (u % 2), HALF * (u % 2 + 1))
                    dve.tensor_scalar(XN[:, c, cs], X[:, c, cs], g[:, 5, c:c + 1], g[:, 6, c:c + 1],
                                      ALU.mult, ALU.add).then_inc(xn_ready, 1)

            def unit_stats(u):
                dve.bn_stats(stats[:, u // 2, u % 2, :],
                             X[:, u // 2, HALF * (u % 2):HALF * (u % 2 + 1)]).then_inc(stats_in, 1)

            for l in range(LAYERS):
                if l:
                    group_norm(l)
                n_units = len(UNITS[l])
                late = set(LATE[l].values())
                for n in range(n_units):
                    if UNITS[l][n][0] != "v" and n not in late:
                        split(l, n)
                for a in range(0, LEAD[l], 2):
                    for i in range(2 * a, 2 * a + 4):
                        maxima(l, i)
                    if a + 2 == TILES:
                        max_rows(l, 0)
                for s in range(0, STEPS, 2):
                    for i in range(2 * (s + LEAD[l]), 2 * (s + LEAD[l]) + 4):
                        if i < 2 * STEPS:
                            maxima(l, i)
                        if i % 4 == 1 and s % TILES == ROWS_STEP[l] and s // TILES + 1 < NH:
                            max_rows(l, s // TILES + 1)
                        if l and i % 4 == 2 and s and s % TILES == 0:
                            even_numerators(l, s // TILES - 1)
                    if l and s > TILES and s % TILES == 2:
                        even_denominators(l, s // TILES - 1)
                    for s1 in (s, s + 1):
                        after = s1 - LAG - 5
                        pair, part = after // (2 * TILES) - 1, after % (2 * TILES)
                        if 0 <= pair and part < REC_PARTS:
                            reciprocals(l, pair, part)
                last_heads(l)
                if l == 0:
                    link(dve.tensor_copy(obias[:, :], col[:, B_PROJ[0][0]:B_PROJ[0][1] + 1]))
                else:
                    dve.wait_ge(vb_done, l)
                    link(dve.tensor_tensor(obias[:, :], M[:, 0:2], col[:, B_PROJ[l][0]:B_PROJ[l][1] + 1], ALU.add))
                for i, u in enumerate(UNIT_ORDER):
                    c, half = u // 2, u % 2
                    cs = slice(HALF * half, HALF * (half + 1))
                    dve.wait_ge(out_done, 4 * l + i + 1)
                    dve.scalar_tensor_tensor(out=X[:, c, cs], in0=S[:, u, :], scalar=obias[:, c:c + 1],
                                             in1=X[:, c, cs], op0=ALU.add, op1=ALU.add).then_inc(x_ready, 1)
                    if l == 1 and i:
                        dve.wait_ge(x_ready, 4 * l + i)
                        unit_stats(UNIT_ORDER[i - 1])
                dve.wait_ge(x_ready, 4 * (l + 1))
                if l == 1:
                    unit_stats(UNIT_ORDER[3])
                if l == 0:
                    for i, u in enumerate(UNIT_ORDER):
                        c, half = u // 2, u % 2
                        cs = slice(HALF * half, HALF * (half + 1))
                        dve.wait_ge(ln_done, half + 1)
                        dve.tensor_tensor(att[:, c, cs], X[:, c, cs], S[:, 4 + half, :], ALU.subtract).then_inc(ln_in, 1)
                    dve.wait_ge(sd_ready, 1)
                    dve.reciprocal(rstd8[:, 1, :], rstd8[:, 0, :]).then_inc(rstd_ready, 1)
                    dve.wait_ge(ln_in, 4)
                    for i, u in enumerate(UNIT_ORDER):
                        c, half = u // 2, u % 2
                        cs = slice(HALF * half, HALF * (half + 1))
                        dve.wait_ge(ln_done, 4 + half)
                        dve.tensor_tensor(X[:, c, cs], att[:, c, cs], B[:, half, :], ALU.mult).then_inc(ln_scaled, 1)
                        if i >= 2:
                            dve.wait_ge(ln_out, i - 1)
                            unit_stats(UNIT_ORDER[i - 2])
                    for i in (2, 3):
                        dve.wait_ge(ln_out, i + 1)
                        unit_stats(UNIT_ORDER[i])
            dve.wait_ge(row_in, 16)
            dve.tensor_reduce(fold[:, :], ident[:, :].rearrange("p (g d) -> p d g", d=L3_DIM), AX.X, ALU.add).then_inc(fold_set, 1)
            for t in range(TILES):
                b = t % 2
                dve.wait_ge(t_done, t + 1)
                dve.tensor_tensor(QK[:, t, :], S[:, QKS_BANK[b], 0:2 * P], bias3[:, 0:2 * P], ALU.add).then_inc(dve_chain, 1)
                chain[0] += 1
                dve.tensor_tensor(QS[:, t, :], S[:, QKS_BANK[b], 2 * P:L3_QKS], bias3[:, 2 * P:L3_QKS],
                                  ALU.add).then_inc(t_used, 1)
                dve.wait_ge(dve_chain, chain[0])
                link(dve.tensor_tensor(QK_prod[:, t, :], QK[:, t, 0:P], QK[:, t, P:2 * P], ALU.mult))
                dve.tensor_reduce(gate[:, 0, t:t + 1], QK_prod[:, t, :], AX.X, ALU.add).then_inc(gate_sums, 1)
            dve.wait_ge(gate_exp, 1)
            link(dve.tensor_scalar(gate[:, 2, :], gate[:, 1, :], 1.0, None, ALU.add))
            link(dve.reciprocal(gate[:, 3, :], gate[:, 2, :]))
            dve.wait_ge(t_used, TILES)
            dve.tensor_tensor(QS, QS, gate[:, 3, :].rearrange("p (t o) -> p t o", o=1).to_broadcast([P, TILES, L3_DIM]),
                              ALU.mult).then_inc(qs_ready, 1)
            dve.wait_ge(parts_done, 1)
            dve.tensor_copy(G_parts, PV[:, 0:C + 1]).then_inc(parts_used, 1)

            def key_low(half):
                cs = slice(HALF * half, HALF * (half + 1))
                mid = slice(L3_DIM, 2 * L3_DIM)
                dve.wait_ge(ke_used, 2 * (half + 1))
                dve.tensor_tensor(ke_stack[mid, cs], Ke[:, cs], ke_stack[mid, cs].bitcast(F32),
                                  ALU.subtract).then_inc(ke_ready, 1)

            dve.wait_ge(G_done, 1)
            dve.tensor_copy(G_sb[:, 0:2 * L3_DIM], M[:, 0:2 * L3_DIM]).then_inc(G_used, 1)
            dve.tensor_copy(G_sb[0:1, 2 * L3_DIM:], M[0:1, 2 * L3_DIM:3 * L3_DIM]).then_inc(G_used, 1)
            dve.wait_ge(en_done, 1)
            dve.tensor_reduce(esum[:, 0, :], M[:, P:P + KC * L3_DIM].rearrange("p (c d) -> p c d", c=KC), AX.X, ALU.max,
                              negate=True).then_inc(max_ready, 1)
            key_low(0)
            dve.wait_ge(en_exp, 2)
            link(dve.reciprocal(esum[:, 2, :], esum[:, 1, :]))
            for c in range(KC):
                dve.tensor_scalar(soft[:, c, :, :], energy[:, c:c + 1, :].to_broadcast([P, 3, L3_DIM]), esum[:, 2, c:c + 1],
                                  None, ALU.mult).then_inc(soft_ready, 1)
            key_low(1)
            dve.wait_ge(at_done, 1)
            dve.tensor_copy(at_stack, M[0:L3_STACK, C:2 * C]).then_inc(at_ready, 1)
            dve.wait_ge(at_ready, 1)
            low = slice(2 * L3_DIM, L3_STACK)
            dve.tensor_tensor(at_stack[low, :], M[low, C:2 * C], at_stack[low, :].bitcast(F32),
                              ALU.subtract).then_inc(at_ready, 1)
            for u in (0, 2):
                dve.wait_ge(vo_done, u + 1)
                dve.tensor_copy(XN[:, u // 2, 0:HALF], S[:, FINAL[u], :]).then_inc(fin_dve, 1)

        @block.tensor
        def _(pe):
            def keep_warm(n):
                for _ in range(n):
                    pe.matmul(PV[:, 0:P], ones[:, :], ones[:, :], start=True, stop=True)

            def projection(l, n, chunks=range(KC)):
                kind, c, half = UNITS[l][n]
                u = UNIT0[l] + n
                src = X if l == 0 else XN
                if n >= RING and (0 in chunks or kind == "v"):
                    pe.wait_ge(proj_used, u - RING + 1)

                if kind == "v":
                    t, tiles = c, half
                    wide = HALF // tiles
                    for j in range(tiles):
                        for kc in range(KC):
                            mm = pe.matmul(B[:, u % RING, wide * j:wide * (j + 1)],
                                           src[:, kc, P * (t + j):P * (t + j + 1)],
                                           W[l][:, kc, 2 * wide:3 * wide], start=(kc == 0), stop=(kc == KC - 1))
                else:
                    wide = P if l == 0 else C
                    off = (0 if kind == "q" else wide) + P * c
                    for kc in chunks:
                        mm = pe.matmul(B[:, u % RING, :], W[l][:, kc, off:off + P],
                                       src[:, kc, HALF * half:HALF * (half + 1)],
                                       start=(kc == 0), stop=(kc == KC - 1))
                if KC - 1 in chunks:
                    mm.then_inc(proj_done, 1)

            def scores_for_max(l, i):
                h, t, half = score_unit(i)
                u = 2 * l * STEPS + i
                if t == 0 and half == 0:
                    pe.wait_ge(stack_dma[h], stack_count(l))
                if u >= RING:
                    pe.wait_ge(a_used, u - RING + 1)
                pe.matmul(A[:, u % RING, :], q_stack[0:SHIFT_ROW, h, P * t:P * (t + 1)],
                          k_stack[0:SHIFT_ROW, h, HALF * half:HALF * (half + 1)],
                          start=True, stop=True).then_inc(a_done, 1)

            def transpose_max(l, h):
                n = l * NH + h
                pe.wait_ge(negmax_ready, n + 1)
                if n:
                    pe.wait_ge(rows_used, 2 * n)
                if l == 0 and h >= 3:
                    pe.wait_ge(pv_used, 2 * (h - 2))
                if l and h:
                    pe.wait_ge(pv_used, 2 * (n - 1))
                pe.transpose(M[0:TILES, 0:P], negmax[:, n % 2, :], ident[:, :]).then_inc(rows_done, 1)

            def scores(l, i):
                h, t, half = score_unit(i)
                v = 2 * l * STEPS + i
                if t == 0 and half == 0:
                    n = l * NH + h
                    pe.wait_ge(shift_dma[n % 2], 32 * (n // 2 + 1))
                if v >= RING:
                    pe.wait_ge(e_ready, v - RING + 1)
                pe.matmul(B[:, v % RING, :], k_stack[:, h, P * t:P * (t + 1)],
                          q_stack[:, h, HALF * half:HALF * (half + 1)],
                          start=True, stop=True).then_inc(b_done, 1)

            def values(l, s):
                g, h, t = l * STEPS + s, s // TILES, s % TILES
                n = l * NH + h
                if t == 0 and h + l:
                    if l == 0:
                        pe.wait_ge(sums_ready, h)
                    else:
                        pe.wait_ge(pv_used, 2 * n - 1)
                pe.wait_ge(e_ready, 2 * (g + 2))
                for r in range(4):
                    tile, half = r // 2, r % 2
                    mm = pe.matmul(PV[DP * r:DP * (r + 1), :], V[:, t + tile, DP * h:DP * (h + 1)],
                                   E[:, (g + tile) % E_BUFS, HALF * half:HALF * (half + 1)],
                                   start=(t == 0), stop=(t == TILES - 2))
                mm.then_inc(pv_done, 2)

            def denominators(l, h, part):
                n = l * NH + h
                last = h == NH - 1 and part == 1
                if part == 0:
                    pe.wait_ge(rows_used, 2 * min(n + 2, (l + 1) * NH))
                    pe.wait_ge(pv_used, 2 * n)
                pe.wait_ge(sum_ready, sum_count(l, 4 * h + 2 * part + (0 if last else 1)))
                groups = [(E_sum[2 * part + r // 2][:, HALF * (r % 2):HALF * (r % 2 + 1)], r) for r in range(2 if last else 4)]
                if last:
                    g = (l + 1) * STEPS - 2
                    groups += [(E[:, (g + r // 2) % E_BUFS, HALF * (r % 2):HALF * (r % 2 + 1)], r) for r in range(4)]
                for k, (rhs, r) in enumerate(groups):
                    mm = pe.matmul(M[DP * r:DP * (r + 1), :], ones[:, 0:DP], rhs, start=(part == 0),
                                   stop=(part == 1 and k >= len(groups) - 4))
                mm.then_inc(den_done, 1)

            def gather_sums(h):
                pe.wait_ge(sums_ready, h + 1)
                pe.wait_ge(rows_used, 2 * min(h + 3, NH))
                if h:
                    pe.wait_ge(pv_used, 2 * h)
                pe.matmul(M[:, :], gather[:, :], sums_sb[:, :], start=True, stop=True).then_inc(gathered, 1)

            pe.wait_ge(ones_set, 1)
            keep_warm(18)
            for l in range(LAYERS):
                pe.wait_ge(w_in[l], 16)
                if l == 0:
                    pe.wait_ge(x_in[0], 16)
                else:
                    keep_warm(14)
                    pe.wait_ge(stat_ready, 3 * l - 1)
                    pe.matmul(M[:, 2:4], group_avg[:, :], mv[:, :, 0], start=True, stop=True).then_inc(stat_done, 1)
                    keep_warm(3)
                    pe.wait_ge(stat_ready, 3 * l)
                    pe.matmul(M[:, 4:6], group_avg[:, :], gsmall[:, 3, :], start=True, stop=True).then_inc(stat_done, 1)
                    keep_warm(6)
                    pe.wait_ge(xn_ready, 4 * (l - 1) + 2)
                late = set(LATE[l].values())
                for n in range(len(UNITS[l])):
                    if n == 1:
                        if l:
                            pe.wait_ge(xn_ready, 4 * l)
                        else:
                            pe.wait_ge(x_in[1], 16)
                    if n == 4 and l == 0:
                        pe.wait_ge(w_v, 16)
                    if n not in late:
                        projection(l, n)
                if l == 0:
                    keep_warm(4)
                    pe.wait_ge(const_set, 6)
                    pe.wait_ge(one_rows_in, 48)
                    pe.wait_ge(pos_rows, 16 * 4)
                for a in range(0, LEAD[l], 2):
                    for i in range(2 * a, 2 * a + 4):
                        scores_for_max(l, i)
                        tile = i // 2
                        if i % 2 and tile + 1 in LATE[l] and UNITS[l][LATE[l][tile + 1]][0] != "v":
                            projection(l, LATE[l][tile + 1], (0,))
                        if i % 2 and tile in LATE[l]:
                            projection(l, LATE[l][tile], (1,))
                    if a + 2 == TILES:
                        transpose_max(l, 0)
                pe.wait_ge(proj_used, UNIT0[l] + len(UNITS[l]))
                for s in range(0, STEPS, 2):
                    rows_now = s % TILES == ROWS_STEP[l] and s // TILES + 1 < NH
                    for i in range(2 * s, 2 * s + 4):
                        if i + 2 * LEAD[l] < 2 * STEPS:
                            scores_for_max(l, i + 2 * LEAD[l])
                        scores(l, i)
                        if i % 4 == 1 and s >= LAG:
                            values(l, s - LAG)
                        if i % 4 == 1:
                            if rows_now:
                                transpose_max(l, s // TILES + 1)
                            if l == 0 and s % TILES == 4 and s > TILES:
                                gather_sums(s // TILES - 1)
                            if l and s % TILES == 2 and s > TILES:
                                denominators(l, s // TILES - 1, 1)
                            if s % TILES == 6 and l:
                                denominators(l, s // TILES, 0)
                values(l, STEPS - LAG)
                if l == 0:
                    gather_sums(NH - 1)
                else:
                    denominators(l, NH - 1, 1)
                wo = (W_COLS[l] - C)
                pe.wait_ge(e_ready, 2 * STEPS * (l + 1))
                pe.wait_ge(a_used, 2 * STEPS * (l + 1))
                for kc in range(KC):
                    if l and kc:
                        pe.wait_ge(pv_used, 2 * (l + 1) * NH)
                        for c in range(KC):
                            for k in range(KC):
                                mm = pe.matmul(M[:, c:c + 1], W[l][:, k, wo + P * c:wo + P * (c + 1)],
                                           col[:, BV[l][k]:BV[l][k] + 1], start=(k == 0), stop=(k == KC - 1))
                        mm.then_inc(vb_done, 1)
                    pe.wait_ge(att_ready, 2 * (l * NH + 4 * (kc + 1)))
                    if kc == KC - 1:
                        pe.wait_ge(att_tail, 2 * (l + 1))
                    for u in UNIT_ORDER:
                        c, half = u // 2, u % 2
                        mm = pe.matmul(S[:, u, :], W[l][:, kc, wo + P * c:wo + P * (c + 1)],
                                       att[:, kc, HALF * half:HALF * (half + 1)], start=(kc == 0), stop=(kc == KC - 1))
                        if kc == KC - 1:
                            mm.then_inc(out_done, 1)
                if l == 0:
                    for half in range(2):
                        pe.wait_ge(x_ready, 2 * (half + 1))
                        for kc in range(KC):
                            mm = pe.matmul(S[:, 4 + half, :], chan_avg[:, :], X[:, kc, HALF * half:HALF * (half + 1)],
                                           start=(kc == 0), stop=(kc == KC - 1))
                        mm.then_inc(ln_done, 1)
                    for t in range(TILES):
                        if t % 4 == 0:
                            pe.wait_ge(sq_ready, 2 + 2 * (t // 4))
                        for kc in range(KC):
                            mm = pe.matmul(M[:, 8 + t:9 + t], XN[:, kc, P * t:P * (t + 1)], chan_avg[:, 0:1],
                                           start=(kc == 0), stop=(kc == KC - 1))
                    mm.then_inc(ln_done, 1)
                    pe.wait_ge(rstd_ready, 1)
                    for t in range(TILES):
                        mm = pe.matmul(B[:, t // 4, P * (t % 4):P * (t % 4 + 1)],
                                       rstd8[:, 1, t:t + 1].to_broadcast([P, P]), ident[:, :], start=True, stop=True)
                        if t % 4 == 3:
                            mm.then_inc(ln_done, 1)
            def keys(half, kc):
                mm = pe.matmul(S[0:L3_STACK, KE_BANK[half], :], W3[:, kc, L3_COLS:L3_COLS + L3_STACK],
                               X[:, kc, HALF * half:HALF * (half + 1)], start=(kc == 0), stop=(kc == KC - 1))
                if kc == KC - 1:
                    mm.then_inc(ke_done, 1)

            def residual(u):
                pe.matmul(S[:, FINAL[u], :], ident[:, :], X[:, u // 2, HALF * (u % 2):HALF * (u % 2 + 1)],
                          start=True, stop=False)

            pe.wait_ge(w_in[3], 16)
            for t in range(TILES):
                b = t % 2
                if t % 4 == 0:
                    pe.wait_ge(x_ready, 4 * LAYERS - (2 if t == 0 else 0))
                if t >= 2:
                    pe.wait_ge(t_used, t - 1)
                for kc in range(KC):
                    mm = pe.matmul(S[:, QKS_BANK[b], 0:L3_QKS], X[:, kc, P * t:P * (t + 1)], W3[:, kc, 0:L3_QKS],
                                   start=(kc == 0), stop=(kc == KC - 1))
                mm.then_inc(t_done, 1)
                if t >= 2:
                    pe.wait_ge(xt_used, t)
                for kc in range(KC):
                    mm = pe.transpose(S[:, XT_BANK[b], P * kc:P * (kc + 1)], X[:, kc, P * t:P * (t + 1)], ident[:, :])
                mm.then_inc(xt_done, 1)
            for kc in range(KC):
                keys(0, kc)
            pe.wait_ge(qs_ready, 1)
            pe.wait_ge(xt_used, TILES + 1)
            for t in range(TILES):
                r = L3_DIM * (t % 4)
                mm = pe.matmul(PV[r:r + L3_DIM, 0:C + 1], QS[:, t, :], XT[:, t, :], start=(t < 4), stop=(t >= 4))
            mm.then_inc(parts_done, 1)
            keys(1, 0)
            pe.wait_ge(parts_used, 1)
            pe.wait_ge(fold_set, 1)
            for kc in range(KC):
                pe.matmul(M[:, L3_DIM * kc:L3_DIM * (kc + 1)], G_parts[:, P * kc:P * (kc + 1)], fold[:, :],
                          start=True, stop=True)
            pe.matmul(M[0:1, 2 * L3_DIM:3 * L3_DIM], G_parts[:, C:C + 1], fold[:, :],
                      start=True, stop=True).then_inc(G_done, 1)
            keys(1, 1)
            pe.wait_ge(G_used, 2)
            for c in range(KC):
                out_cols = M[:, P + L3_DIM * c:P + L3_DIM * (c + 1)]
                for kc in range(KC):
                    pe.matmul(out_cols, W3[:, kc, L3_QKS + P * c:L3_QKS + P * (c + 1)],
                              G_sb[:, L3_DIM * kc:L3_DIM * (kc + 1)], start=(kc == 0), stop=False)
                mm = pe.matmul(out_cols, bias3[0:1, L3_QKS + P * c:L3_QKS + P * (c + 1)], G_sb[0:1, 2 * L3_DIM:],
                               start=False, stop=True)
            mm.then_inc(en_done, 1)
            pe.wait_ge(t_used, TILES)
            for u in range(2):
                residual(u)
            pe.wait_ge(soft_ready, KC)
            for c in range(KC):
                mm = pe.transpose(M[0:L3_STACK, C + P * c:C + P * (c + 1)],
                                  soft[:, c, :, :].rearrange("p r d -> p (r d)"), ident[:, :])
            mm.then_inc(at_done, 1)
            for u in range(2, 4):
                residual(u)
            pe.wait_ge(at_ready, 2)
            pe.wait_ge(ke_ready, 2)
            for u in range(4):
                c, half = u // 2, u % 2
                pe.matmul(S[:, FINAL[u], :], at_stack[:, P * c:P * (c + 1)], ke_stack[:, HALF * half:HALF * (half + 1)],
                          start=False, stop=True).then_inc(vo_done, 1)


def kernel(**inputs):
    import numpy as np
    from concourse import bacc
    from concourse.bass_utils import run_bass_kernel_spmd

    g = {k: np.ascontiguousarray(v) for k, v in inputs.items()}

    def chunks(w):
        return np.ascontiguousarray(w.reshape(KC, P, -1).transpose(1, 0, 2))

    wp0 = np.zeros((NH, DP, C), np.float32)
    wp0[:, 0:16] = g["L0_conv_w_proj"].T.reshape(NH, 16, C)
    w0 = chunks(np.concatenate([g["L0_conv_w_qkv"].T, wp0.reshape(NH * DP, C)], 1))
    w1 = chunks(np.concatenate([g[f"L1_conv_w{n}"].T for n in "qkvo"], 1))
    w2 = chunks(np.concatenate([g["L2_conv_w_qkv"].T, g["L2_conv_w_proj"].T], 1))
    w3 = chunks(np.concatenate([g[f"L3_conv_W{n}"].T for n in "qksveee"], 1))
    vectors = [g["L0_conv_b_proj"], g["L0_conv_gamma"], g["L0_conv_beta"],
               g["L1_conv_bq"], g["L1_conv_bk"], g["L1_conv_bv"],
               g["L1_conv_bo"], g["L1_conv_gn_gamma"], g["L1_conv_gn_beta"],
               g["L2_conv_b_qkv"][0:C], g["L2_conv_b_qkv"][C:2 * C], g["L2_conv_b_qkv"][2 * C:],
               g["L2_conv_b_proj"], g["L2_conv_gamma"], g["L2_conv_beta"]]
    cols = np.zeros((P, 40), np.float32)
    for i, v in enumerate(vectors):
        cols[:, 2 * i:2 * i + 2] = v.reshape(KC, P).T
    cols[0:L3_STACK, 30] = np.tile(g["L3_conv_be"], 3)
    row3 = np.concatenate([g[f"L3_conv_b{n}"] for n in "qksv"])[None, :]
    arrays = {"x_in_dram": g["x"].reshape(KC, P, N), "w0_dram": w0, "w1_dram": w1, "w2_dram": w2, "w3_dram": w3,
              "pos_dram": g["L0_conv_pos_bias"], "cols_dram": cols, "row3_dram": row3}
    nc = bacc.Bacc("TRN2", target_bir_lowering=False, num_devices=1)
    args = [nc.dram_tensor(n, a.shape, mybir.dt.from_np(a.dtype), kind="ExternalInput").ap() for n, a in arrays.items()]
    out = nc.dram_tensor("out_dram", (KC, P, N), F32, kind="ExternalOutput").ap()
    attention_chain(nc, *args, out)
    r = run_bass_kernel_spmd(nc, [arrays], core_ids=[0])
    return r.results[0]["out_dram"].reshape(1, C, 32, 32)
```
